# Optimizing a Trainium2 kernel written in Bass

```python
import numpy as np
import jax
import jax.numpy as jnp

def _softmax(x, axis=-1):
    return jax.nn.softmax(x, axis=axis)

def _gelu(x):
    return jax.nn.gelu(x, approximate=True)

def _silu(x):
    return jax.nn.silu(x)

def _sigmoid(x):
    return jax.nn.sigmoid(x)

def _layernorm(x, axis=-1, eps=1e-05):
    m = jnp.mean(x, axis=axis, keepdims=True)
    v = jnp.var(x, axis=axis, keepdims=True)
    return (x - m) / jnp.sqrt(v + eps)

def _scatter_add(tgt, idx, src, axis=0):
    return tgt.at[idx].add(src)

def _segment_sum(src, seg, n):
    return jax.ops.segment_sum(src, seg, n)
kernel_name = 'mk_decoder_preln_d2_seqx_r8_0bd736'

def setup_inputs(seed: int=0):
    np.random.seed(seed)
    _w = jnp.asarray

    def _rec_inputs():
        import jax
        import jax.numpy as jnp
        _rk = jax.random.key(seed)
        x = -0.0002928 + 1 * jax.random.normal(jax.random.fold_in(_rk, 1), (16, 256, 128), jnp.float32)
        _lenS = 256 - jax.random.randint(jax.random.fold_in(_rk, 7), (16,), 0, max(1, 256 // 4) + 1, jnp.int32)
        _lenS2 = 64 - jax.random.randint(jax.random.fold_in(_rk, 8), (16,), 0, max(1, 64 // 4) + 1, jnp.int32)
        _ctx_512P = jax.random.normal(jax.random.fold_in(_rk, 11), (16, 16, 64), jnp.float32)
        _ctx_512c = jax.random.dirichlet(jax.random.fold_in(_rk, 511), 0.3 * jnp.ones((16,), jnp.float32), (16, 64))
        _ctx_512t = jnp.einsum('bsk,bkd->bsd', _ctx_512c, _ctx_512P)
        _ctx_512t = _ctx_512t * jax.lax.rsqrt(jnp.mean(jnp.square(_ctx_512t)) + 1e-12) * 0.953939
        ctx_512 = 0.00222621 + 0.99962 * (_ctx_512t + 0.3 * jax.random.normal(jax.random.fold_in(_rk, 611), (16, 64, 64), jnp.float32))
        return (x, ctx_512)
    x, ctx_512 = _rec_inputs()

    def _L0_attn_setup():
        import jax, jax.numpy as jnp
        import numpy as np
        DIM = 128
        D_STATE = 16
        D_CONV = 4
        D_INNER = 2 * DIM
        DT_RANK = (DIM + 15) // 16
        E = 8
        K = 2
        HID = 4 * DIM
        B, L = (1, 256)

        def _rmsnorm(x):
            n = jnp.sqrt(jnp.sum(x * x, axis=-1, keepdims=True))
            return x * DIM ** 0.5 / jnp.maximum(n, 1e-12)

        def _selective_scan(u, A_log, D, x_proj_w, dt_proj_w, dt_proj_b):
            A = -jnp.exp(A_log)
            x_dbl = u @ x_proj_w.T
            dt, Bm, Cm = jnp.split(x_dbl, [DT_RANK, DT_RANK + D_STATE], axis=-1)
            delta = jax.nn.softplus(dt @ dt_proj_w.T + dt_proj_b)
            dA = jnp.exp(delta[..., None] * A)
            dBu = delta[..., None] * Bm[:, :, None, :] * u[..., None]

            def step(h, inp):
                dA_t, dBu_t, C_t = inp
                h = dA_t * h + dBu_t
                y = jnp.einsum('bdn,bn->bd', h, C_t)
                return (h, y)
            h0 = jnp.zeros((u.shape[0], D_INNER, D_STATE), u.dtype)
            _, ys = jax.lax.scan(step, h0, (dA.swapaxes(0, 1), dBu.swapaxes(0, 1), Cm.swapaxes(0, 1)))
            y = ys.swapaxes(0, 1)
            return y + u * D

        def _mamba(xn, in_proj_w, conv_w, conv_b, x_proj_w, dt_proj_w, dt_proj_b, A_log, D, out_proj_w):
            xr = xn @ in_proj_w.T
            xm, res = jnp.split(xr, 2, axis=-1)
            xc = jax.lax.conv_general_dilated(xm.swapaxes(1, 2), conv_w, (1,), [(D_CONV - 1, 0)], feature_group_count=D_INNER) + conv_b[:, None]
            xc = jax.nn.silu(xc.swapaxes(1, 2))
            y = _selective_scan(xc, A_log, D, x_proj_w, dt_proj_w, dt_proj_b)
            y = y * jax.nn.silu(res)
            return y @ out_proj_w.T

        def _moe(x, gate_w, w1, w2):
            gates = jax.nn.softmax(x @ gate_w.T, axis=-1)
            vals, idx = jax.lax.top_k(gates, K)
            vals = vals / jnp.sum(vals, axis=-1, keepdims=True)
            sparse = jnp.sum(jax.nn.one_hot(idx, E, dtype=x.dtype) * vals[..., None], axis=-2)
            h = jax.nn.gelu(jnp.einsum('bld,ehd->bleh', x, w1), approximate=False)
            y = jnp.einsum('bleh,edh->bled', h, w2)
            return jnp.einsum('bled,ble->bld', y, sparse)
        key = jax.random.key(seed)
        ks = jax.random.split(key, 12)
        g = lambda k, shape, s: jax.random.normal(k, shape, jnp.float32) * s
        A_log = jnp.log(jnp.tile(jnp.arange(1, D_STATE + 1, dtype=jnp.float32), (D_INNER, 1)))
        return {'x': g(ks[0], (B, L, DIM), 1.0), 'in_proj_w': g(ks[1], (2 * D_INNER, DIM), 0.02), 'conv_w': g(ks[2], (D_INNER, 1, D_CONV), 0.1), 'conv_b': jnp.zeros((D_INNER,), jnp.float32), 'x_proj_w': g(ks[3], (DT_RANK + 2 * D_STATE, D_INNER), 0.02), 'dt_proj_w': g(ks[4], (D_INNER, DT_RANK), 0.02), 'dt_proj_b': g(ks[5], (D_INNER,), 0.1), 'A_log': A_log, 'D': jnp.ones((D_INNER,), jnp.float32), 'out_proj_w': g(ks[6], (DIM, D_INNER), 0.02), 'gate_w': g(ks[7], (E, DIM), 0.02), 'w1': g(ks[8], (E, HID, DIM), 0.02), 'w2': g(ks[9], (E, DIM, HID), 0.02)}
    _L0_attn_all = _L0_attn_setup()
    _L0_attn_in = {k: v for k, v in _L0_attn_all.items() if k in ('in_proj_w', 'conv_w', 'conv_b', 'x_proj_w', 'dt_proj_w', 'dt_proj_b', 'A_log', 'D', 'out_proj_w', 'gate_w', 'w1', 'w2')}
    del _L0_attn_all

    def _L0_xattn_setup():
        import jax, jax.numpy as jnp
        import numpy as np
        B, T, TC, C, CC, H = (2, 256, 64, 128, 64, 16)
        D = C // H

        def _heads(t):
            b, l, _ = t.shape
            return t.reshape(b, l, H, D).transpose(0, 2, 1, 3)
        key = jax.random.key(seed)
        ks = jax.random.split(key, 18)
        w = lambda k, i, o: jax.random.normal(k, (i, o), jnp.float32) / np.sqrt(i).astype(np.float32)
        return {'x': jax.random.normal(ks[0], (B, T, C), jnp.float32), 'cross_input': jax.random.normal(ks[1], (B, TC, CC), jnp.float32), 'Wk': w(ks[2], C, C), 'bk': jnp.zeros((C,), jnp.float32), 'Wq': w(ks[3], C, C), 'bq': jnp.zeros((C,), jnp.float32), 'Wv': w(ks[4], C, C), 'bv': jnp.zeros((C,), jnp.float32), 'Wck': w(ks[5], CC, C), 'bck': jnp.zeros((C,), jnp.float32), 'Wcq': w(ks[6], C, C), 'bcq': jnp.zeros((C,), jnp.float32), 'Wcv': w(ks[7], CC, C), 'bcv': jnp.zeros((C,), jnp.float32), 'Wp': w(ks[8], C, C), 'bp': jnp.zeros((C,), jnp.float32)}
    _L0_xattn_all = _L0_xattn_setup()
    _L0_xattn_in = {k: v for k, v in _L0_xattn_all.items() if k in ('Wk', 'bk', 'Wq', 'bq', 'Wv', 'bv', 'Wck', 'bck', 'Wcq', 'bcq', 'Wcv', 'bcv', 'Wp', 'bp')}
    del _L0_xattn_all

    def _L0_ffn_setup():
        import jax, jax.numpy as jnp
        import numpy as np
        QMAX = 127.0

        def _ste_round(v):
            return v + jax.lax.stop_gradient(jnp.round(v) - v)

        def _act_fake_quant(x, clip_factor):
            scale = jax.nn.sigmoid(clip_factor) * jnp.max(jnp.abs(x)) / QMAX
            return jnp.clip(_ste_round(x / scale), -QMAX - 1.0, QMAX) * scale

        def _weight_fake_quant(w):
            scale = jnp.max(jnp.abs(w), axis=1, keepdims=True) / QMAX
            return jnp.clip(_ste_round(w / scale), -QMAX - 1.0, QMAX) * scale
        key = jax.random.key(seed)
        k1, k2, k3, k4 = jax.random.split(key, 4)
        B, S, H, I = (8, 1024, 128, 352)
        return {'x': jax.random.normal(k1, (B, S, H), dtype=jnp.float32), 'clip_x': jnp.full((1,), 4.0, dtype=jnp.float32), 'clip_down': jnp.full((1,), 4.0, dtype=jnp.float32), 'w_gate': jax.random.normal(k2, (I, H), dtype=jnp.float32) * 0.02, 'w_up': jax.random.normal(k3, (I, H), dtype=jnp.float32) * 0.02, 'w_down': jax.random.normal(k4, (H, I), dtype=jnp.float32) * 0.02}
    _L0_ffn_all = _L0_ffn_setup()
    _L0_ffn_in = {k: v for k, v in _L0_ffn_all.items() if k in ('clip_x', 'clip_down', 'w_gate', 'w_up', 'w_down')}
    del _L0_ffn_all

    def _L1_attn_setup():
        import jax, jax.numpy as jnp
        import numpy as np
        import math
        B, T, D = (4, 512, 128)
        K, H, KH, C = (64, 4, 16, 64)
        MLP = 512
        EPS = 1e-05

        def _layernorm(x, g, b):
            m = jnp.mean(x, axis=-1, keepdims=True)
            v = jnp.mean((x - m) ** 2, axis=-1, keepdims=True)
            return (x - m) / jnp.sqrt(v + EPS) * g + b

        def _chunked_eigenstate(log_decay, frequency, beta_r, beta_i):
            Bt, Tt, Kt = beta_r.shape
            T_pad = (Tt + C - 1) // C * C
            if T_pad > Tt:
                beta_r = jnp.pad(beta_r, ((0, 0), (0, T_pad - Tt), (0, 0)))
                beta_i = jnp.pad(beta_i, ((0, 0), (0, T_pad - Tt), (0, 0)))
            n_chunks = T_pad // C
            mag = jax.nn.sigmoid(log_decay)
            powers = jnp.arange(C, dtype=log_decay.dtype)
            mag_pow = mag[:, None] ** powers[None, :]
            phases = frequency[:, None] * powers[None, :]
            kr = mag_pow * jnp.cos(phases)
            ki = mag_pow * jnp.sin(phases)
            ii = jnp.arange(C)
            idx = ii[None, :] - ii[:, None]
            mask = (idx >= 0).astype(kr.dtype)
            idxc = jnp.clip(idx, 0, C - 1)
            L_r = kr[:, idxc] * mask[None]
            L_i = ki[:, idxc] * mask[None]
            br = beta_r.reshape(Bt, n_chunks, C, Kt)
            bi = beta_i.reshape(Bt, n_chunks, C, Kt)
            intra_r = jnp.einsum('kjs,bnsk->bnjk', L_r, br) - jnp.einsum('kjs,bnsk->bnjk', L_i, bi)
            intra_i = jnp.einsum('kjs,bnsk->bnjk', L_r, bi) + jnp.einsum('kjs,bnsk->bnjk', L_i, br)
            first_col_r = L_r[:, :, 0]
            first_col_i = L_i[:, :, 0]

            def step(carry, intra):
                sr, si = carry
                ir, im = intra
                cr = first_col_r[None] * sr[:, :, None] - first_col_i[None] * si[:, :, None]
                ci = first_col_r[None] * si[:, :, None] + first_col_i[None] * sr[:, :, None]
                o_r = ir + jnp.transpose(cr, (0, 2, 1))
                o_i = im + jnp.transpose(ci, (0, 2, 1))
                return ((o_r[:, -1, :], o_i[:, -1, :]), (o_r, o_i))
            xs = (jnp.transpose(intra_r, (1, 0, 2, 3)), jnp.transpose(intra_i, (1, 0, 2, 3)))
            init = (jnp.zeros((Bt, Kt), beta_r.dtype), jnp.zeros((Bt, Kt), beta_r.dtype))
            _, (out_r, out_i) = jax.lax.scan(step, init, xs)
            c_r = jnp.transpose(out_r, (1, 0, 2, 3)).reshape(Bt, T_pad, Kt)[:, :Tt]
            c_i = jnp.transpose(out_i, (1, 0, 2, 3)).reshape(Bt, T_pad, Kt)[:, :Tt]
            return (c_r, c_i)
        key = jax.random.key(seed)
        ks = jax.random.split(key, 8)

        def n(k, shape, scale):
            return jax.random.normal(k, shape, dtype=jnp.float32) * scale
        return {'x': jax.random.normal(ks[0], (B, T, D), dtype=jnp.float32), 'w_in': n(ks[1], (2 * K, D), D ** (-0.5)), 'w_out': n(ks[2], (D, 2 * K), (2 * K) ** (-0.5)), 'w_gate': n(ks[3], (D, D), D ** (-0.5)), 'b_gate': jnp.full((D,), -2.0, dtype=jnp.float32), 'log_decay': jax.random.uniform(ks[4], (K,), minval=-3.0, maxval=-0.1, dtype=jnp.float32), 'frequency': jnp.linspace(0.0, 2.0 * math.pi * (1.0 - 1.0 / K), K, dtype=jnp.float32), 'coupling': jnp.eye(KH, dtype=jnp.float32)[None] + 0.01 * jax.random.normal(ks[5], (H, KH, KH), dtype=jnp.float32) / math.sqrt(KH), 'w_mlp1': n(ks[6], (MLP, D), D ** (-0.5)), 'b_mlp1': jnp.zeros((MLP,), jnp.float32), 'w_mlp2': n(ks[7], (D, MLP), MLP ** (-0.5)), 'b_mlp2': jnp.zeros((D,), jnp.float32), 'ln1_g': jnp.ones((D,), jnp.float32), 'ln1_b': jnp.zeros((D,), jnp.float32), 'ln2_g': jnp.ones((D,), jnp.float32), 'ln2_b': jnp.zeros((D,), jnp.float32)}
    _L1_attn_all = _L1_attn_setup()
    _L1_attn_in = {k: v for k, v in _L1_attn_all.items() if k in ('w_in', 'w_out', 'w_gate', 'b_gate', 'log_decay', 'frequency', 'coupling', 'w_mlp1', 'b_mlp1', 'w_mlp2', 'b_mlp2', 'ln1_g', 'ln1_b', 'ln2_g', 'ln2_b')}
    del _L1_attn_all

    def _L1_xattn_setup():
        import jax, jax.numpy as jnp
        import numpy as np
        H, D, C1, C2, S, M, B, W = (16, 32, 128, 64, 256, 64, 2, 4)

        def _ln(x, g, b):
            m = jnp.mean(x, -1, keepdims=True)
            v = jnp.var(x, -1, keepdims=True)
            return (x - m) * jax.lax.rsqrt(v + 1e-05) * g + b

        def _mha(x, y, wq, wk, wv, li1_w, li1_b, lnx_g, lnx_b, lny_g, lny_b, ln3_g, ln3_b, li2_w, li2_b, li3_w, li3_b, causal):
            xn = _ln(x, lnx_g, lnx_b)
            yn = _ln(y, lny_g, lny_b)
            q = jnp.einsum('bsc,hcd->bhsd', xn, wq)
            k = jnp.einsum('btc,hcd->bhtd', yn, wk)
            v = jnp.einsum('btc,hcd->bhtd', yn, wv)
            a = jax.nn.softmax(jnp.einsum('bhsd,bhtd->bhst', q, k) * D ** (-0.5), axis=-1)
            if causal:
                s, t = (a.shape[-2], a.shape[-1])
                mask = (jnp.arange(t)[None, :] > jnp.arange(s)[:, None]).astype(a.dtype)
                a = a * mask
            o = jnp.einsum('bhst,bhtd->bhsd', a, v)
            o = o.transpose(0, 2, 1, 3).reshape(x.shape[0], x.shape[1], H * D)
            x_out = x + o @ li1_w + li1_b
            h = jax.nn.gelu(_ln(x_out, ln3_g, ln3_b) @ li2_w + li2_b, approximate=False)
            return x_out + h @ li3_w + li3_b
        key = jax.random.key(seed)
        ks = iter(jax.random.split(key, 64))

        def w(shape, scale=0.02):
            return jax.random.normal(next(ks), shape, jnp.float32) * scale
        inp = {'xx': jax.random.normal(next(ks), (B, S, C1), jnp.float32), 'ee': jax.random.normal(next(ks), (B, M, C2), jnp.float32), 'ln1_g': jnp.ones(C1, jnp.float32), 'ln1_b': jnp.zeros(C1, jnp.float32), 'ln2_g': jnp.ones(C1, jnp.float32), 'ln2_b': jnp.zeros(C1, jnp.float32)}
        for pfx, cy in (('a1', C1), ('a2', C2)):
            inp[pfx + '_wq'] = w((H, C1, D))
            inp[pfx + '_wk'] = w((H, cy, D))
            inp[pfx + '_wv'] = w((H, cy, D))
            inp[pfx + '_li1_w'] = w((H * D, C1))
            inp[pfx + '_li1_b'] = jnp.zeros(C1, jnp.float32)
            inp[pfx + '_lnx_g'] = jnp.ones(C1, jnp.float32)
            inp[pfx + '_lnx_b'] = jnp.zeros(C1, jnp.float32)
            inp[pfx + '_lny_g'] = jnp.ones(cy, jnp.float32)
            inp[pfx + '_lny_b'] = jnp.zeros(cy, jnp.float32)
            inp[pfx + '_ln3_g'] = jnp.ones(C1, jnp.float32)
            inp[pfx + '_ln3_b'] = jnp.zeros(C1, jnp.float32)
            inp[pfx + '_li2_w'] = w((C1, C1 * W))
            inp[pfx + '_li2_b'] = jnp.zeros(C1 * W, jnp.float32)
            inp[pfx + '_li3_w'] = w((C1 * W, C1))
            inp[pfx + '_li3_b'] = jnp.zeros(C1, jnp.float32)
        inp['training'] = 0
        return inp
    _L1_xattn_all = _L1_xattn_setup()
    _L1_xattn_in = {k: v for k, v in _L1_xattn_all.items() if k in ('ln1_g', 'ln1_b', 'ln2_g', 'ln2_b', 'a1_wq', 'a1_wk', 'a1_wv', 'a1_li1_w', 'a1_li1_b', 'a1_lnx_g', 'a1_lnx_b', 'a1_lny_g', 'a1_lny_b', 'a1_ln3_g', 'a1_ln3_b', 'a1_li2_w', 'a1_li2_b', 'a1_li3_w', 'a1_li3_b', 'a2_wq', 'a2_wk', 'a2_wv', 'a2_li1_w', 'a2_li1_b', 'a2_lnx_g', 'a2_lnx_b', 'a2_lny_g', 'a2_lny_b', 'a2_ln3_g', 'a2_ln3_b', 'a2_li2_w', 'a2_li2_b', 'a2_li3_w', 'a2_li3_b')}
    del _L1_xattn_all

    def _L1_ffn_setup():
        import jax, jax.numpy as jnp
        import numpy as np
        B, T, C = (4, 256, 128)
        E, F, K = (8, 256, 2)
        key = jax.random.key(seed)
        k0, k1, k2, k3 = jax.random.split(key, 4)
        s = lambda d: 1.0 / np.sqrt(d)
        x = jax.random.normal(k0, (B, T, C), dtype=jnp.float32)
        Wr = jax.random.normal(k1, (E, C), dtype=jnp.float32) * s(C)
        W1 = jax.random.normal(k2, (E, 2 * F, C), dtype=jnp.float32) * s(C)
        W2 = jax.random.normal(k3, (E, C, F), dtype=jnp.float32) * s(F)
        return {'x': x, 'Wr': Wr, 'W1': W1, 'W2': W2}
    _L1_ffn_all = _L1_ffn_setup()
    _L1_ffn_in = {k: v for k, v in _L1_ffn_all.items() if k in ('Wr', 'W1', 'W2')}
    del _L1_ffn_all
    return {'x': x, 'ctx_512': ctx_512, 'L0_attn_in_proj_w': _L0_attn_in['in_proj_w'], 'L0_attn_conv_w': _L0_attn_in['conv_w'], 'L0_attn_conv_b': _L0_attn_in['conv_b'], 'L0_attn_x_proj_w': _L0_attn_in['x_proj_w'], 'L0_attn_dt_proj_w': _L0_attn_in['dt_proj_w'], 'L0_attn_dt_proj_b': _L0_attn_in['dt_proj_b'], 'L0_attn_A_log': _L0_attn_in['A_log'], 'L0_attn_D': _L0_attn_in['D'], 'L0_attn_out_proj_w': _L0_attn_in['out_proj_w'], 'L0_attn_gate_w': _L0_attn_in['gate_w'], 'L0_attn_w1': _L0_attn_in['w1'], 'L0_attn_w2': _L0_attn_in['w2'], 'L0_xattn_Wk': _L0_xattn_in['Wk'], 'L0_xattn_bk': _L0_xattn_in['bk'], 'L0_xattn_Wq': _L0_xattn_in['Wq'], 'L0_xattn_bq': _L0_xattn_in['bq'], 'L0_xattn_Wv': _L0_xattn_in['Wv'], 'L0_xattn_bv': _L0_xattn_in['bv'], 'L0_xattn_Wck': _L0_xattn_in['Wck'], 'L0_xattn_bck': _L0_xattn_in['bck'], 'L0_xattn_Wcq': _L0_xattn_in['Wcq'], 'L0_xattn_bcq': _L0_xattn_in['bcq'], 'L0_xattn_Wcv': _L0_xattn_in['Wcv'], 'L0_xattn_bcv': _L0_xattn_in['bcv'], 'L0_xattn_Wp': _L0_xattn_in['Wp'], 'L0_xattn_bp': _L0_xattn_in['bp'], 'L0_ffn_clip_x': _L0_ffn_in['clip_x'], 'L0_ffn_clip_down': _L0_ffn_in['clip_down'], 'L0_ffn_w_gate': _L0_ffn_in['w_gate'], 'L0_ffn_w_up': _L0_ffn_in['w_up'], 'L0_ffn_w_down': _L0_ffn_in['w_down'], 'L1_attn_w_in': _L1_attn_in['w_in'], 'L1_attn_w_out': _L1_attn_in['w_out'], 'L1_attn_w_gate': _L1_attn_in['w_gate'], 'L1_attn_b_gate': _L1_attn_in['b_gate'], 'L1_attn_log_decay': _L1_attn_in['log_decay'], 'L1_attn_frequency': _L1_attn_in['frequency'], 'L1_attn_coupling': _L1_attn_in['coupling'], 'L1_attn_w_mlp1': _L1_attn_in['w_mlp1'], 'L1_attn_b_mlp1': _L1_attn_in['b_mlp1'], 'L1_attn_w_mlp2': _L1_attn_in['w_mlp2'], 'L1_attn_b_mlp2': _L1_attn_in['b_mlp2'], 'L1_attn_ln1_g': _L1_attn_in['ln1_g'], 'L1_attn_ln1_b': _L1_attn_in['ln1_b'], 'L1_attn_ln2_g': _L1_attn_in['ln2_g'], 'L1_attn_ln2_b': _L1_attn_in['ln2_b'], 'L1_xattn_ln1_g': _L1_xattn_in['ln1_g'], 'L1_xattn_ln1_b': _L1_xattn_in['ln1_b'], 'L1_xattn_ln2_g': _L1_xattn_in['ln2_g'], 'L1_xattn_ln2_b': _L1_xattn_in['ln2_b'], 'L1_xattn_a1_wq': _L1_xattn_in['a1_wq'], 'L1_xattn_a1_wk': _L1_xattn_in['a1_wk'], 'L1_xattn_a1_wv': _L1_xattn_in['a1_wv'], 'L1_xattn_a1_li1_w': _L1_xattn_in['a1_li1_w'], 'L1_xattn_a1_li1_b': _L1_xattn_in['a1_li1_b'], 'L1_xattn_a1_lnx_g': _L1_xattn_in['a1_lnx_g'], 'L1_xattn_a1_lnx_b': _L1_xattn_in['a1_lnx_b'], 'L1_xattn_a1_lny_g': _L1_xattn_in['a1_lny_g'], 'L1_xattn_a1_lny_b': _L1_xattn_in['a1_lny_b'], 'L1_xattn_a1_ln3_g': _L1_xattn_in['a1_ln3_g'], 'L1_xattn_a1_ln3_b': _L1_xattn_in['a1_ln3_b'], 'L1_xattn_a1_li2_w': _L1_xattn_in['a1_li2_w'], 'L1_xattn_a1_li2_b': _L1_xattn_in['a1_li2_b'], 'L1_xattn_a1_li3_w': _L1_xattn_in['a1_li3_w'], 'L1_xattn_a1_li3_b': _L1_xattn_in['a1_li3_b'], 'L1_xattn_a2_wq': _L1_xattn_in['a2_wq'], 'L1_xattn_a2_wk': _L1_xattn_in['a2_wk'], 'L1_xattn_a2_wv': _L1_xattn_in['a2_wv'], 'L1_xattn_a2_li1_w': _L1_xattn_in['a2_li1_w'], 'L1_xattn_a2_li1_b': _L1_xattn_in['a2_li1_b'], 'L1_xattn_a2_lnx_g': _L1_xattn_in['a2_lnx_g'], 'L1_xattn_a2_lnx_b': _L1_xattn_in['a2_lnx_b'], 'L1_xattn_a2_lny_g': _L1_xattn_in['a2_lny_g'], 'L1_xattn_a2_lny_b': _L1_xattn_in['a2_lny_b'], 'L1_xattn_a2_ln3_g': _L1_xattn_in['a2_ln3_g'], 'L1_xattn_a2_ln3_b': _L1_xattn_in['a2_ln3_b'], 'L1_xattn_a2_li2_w': _L1_xattn_in['a2_li2_w'], 'L1_xattn_a2_li2_b': _L1_xattn_in['a2_li2_b'], 'L1_xattn_a2_li3_w': _L1_xattn_in['a2_li3_w'], 'L1_xattn_a2_li3_b': _L1_xattn_in['a2_li3_b'], 'L1_ffn_Wr': _L1_ffn_in['Wr'], 'L1_ffn_W1': _L1_ffn_in['W1'], 'L1_ffn_W2': _L1_ffn_in['W2']}

def reference(x, ctx_512, L0_attn_in_proj_w, L0_attn_conv_w, L0_attn_conv_b, L0_attn_x_proj_w, L0_attn_dt_proj_w, L0_attn_dt_proj_b, L0_attn_A_log, L0_attn_D, L0_attn_out_proj_w, L0_attn_gate_w, L0_attn_w1, L0_attn_w2, L0_xattn_Wk, L0_xattn_bk, L0_xattn_Wq, L0_xattn_bq, L0_xattn_Wv, L0_xattn_bv, L0_xattn_Wck, L0_xattn_bck, L0_xattn_Wcq, L0_xattn_bcq, L0_xattn_Wcv, L0_xattn_bcv, L0_xattn_Wp, L0_xattn_bp, L0_ffn_clip_x, L0_ffn_clip_down, L0_ffn_w_gate, L0_ffn_w_up, L0_ffn_w_down, L1_attn_w_in, L1_attn_w_out, L1_attn_w_gate, L1_attn_b_gate, L1_attn_log_decay, L1_attn_frequency, L1_attn_coupling, L1_attn_w_mlp1, L1_attn_b_mlp1, L1_attn_w_mlp2, L1_attn_b_mlp2, L1_attn_ln1_g, L1_attn_ln1_b, L1_attn_ln2_g, L1_attn_ln2_b, L1_xattn_ln1_g, L1_xattn_ln1_b, L1_xattn_ln2_g, L1_xattn_ln2_b, L1_xattn_a1_wq, L1_xattn_a1_wk, L1_xattn_a1_wv, L1_xattn_a1_li1_w, L1_xattn_a1_li1_b, L1_xattn_a1_lnx_g, L1_xattn_a1_lnx_b, L1_xattn_a1_lny_g, L1_xattn_a1_lny_b, L1_xattn_a1_ln3_g, L1_xattn_a1_ln3_b, L1_xattn_a1_li2_w, L1_xattn_a1_li2_b, L1_xattn_a1_li3_w, L1_xattn_a1_li3_b, L1_xattn_a2_wq, L1_xattn_a2_wk, L1_xattn_a2_wv, L1_xattn_a2_li1_w, L1_xattn_a2_li1_b, L1_xattn_a2_lnx_g, L1_xattn_a2_lnx_b, L1_xattn_a2_lny_g, L1_xattn_a2_lny_b, L1_xattn_a2_ln3_g, L1_xattn_a2_ln3_b, L1_xattn_a2_li2_w, L1_xattn_a2_li2_b, L1_xattn_a2_li3_w, L1_xattn_a2_li3_b, L1_ffn_Wr, L1_ffn_W1, L1_ffn_W2):
    import jax
    import jax.numpy as jnp

    def _L0_attn_ref(x, in_proj_w, conv_w, conv_b, x_proj_w, dt_proj_w, dt_proj_b, A_log, D, out_proj_w, gate_w, w1, w2):
        import jax, jax.numpy as jnp
        import numpy as np
        DIM = 128
        D_STATE = 16
        D_CONV = 4
        D_INNER = 2 * DIM
        DT_RANK = (DIM + 15) // 16
        E = 8
        K = 2
        HID = 4 * DIM
        B, L = (1, 256)

        def _rmsnorm(x):
            n = jnp.sqrt(jnp.sum(x * x, axis=-1, keepdims=True))
            return x * DIM ** 0.5 / jnp.maximum(n, 1e-12)

        def _selective_scan(u, A_log, D, x_proj_w, dt_proj_w, dt_proj_b):
            A = -jnp.exp(A_log)
            x_dbl = u @ x_proj_w.T
            dt, Bm, Cm = jnp.split(x_dbl, [DT_RANK, DT_RANK + D_STATE], axis=-1)
            delta = jax.nn.softplus(dt @ dt_proj_w.T + dt_proj_b)
            dA = jnp.exp(delta[..., None] * A)
            dBu = delta[..., None] * Bm[:, :, None, :] * u[..., None]

            def step(h, inp):
                dA_t, dBu_t, C_t = inp
                h = dA_t * h + dBu_t
                y = jnp.einsum('bdn,bn->bd', h, C_t)
                return (h, y)
            h0 = jnp.zeros((u.shape[0], D_INNER, D_STATE), u.dtype)
            _, ys = jax.lax.scan(step, h0, (dA.swapaxes(0, 1), dBu.swapaxes(0, 1), Cm.swapaxes(0, 1)))
            y = ys.swapaxes(0, 1)
            return y + u * D

        def _mamba(xn, in_proj_w, conv_w, conv_b, x_proj_w, dt_proj_w, dt_proj_b, A_log, D, out_proj_w):
            xr = xn @ in_proj_w.T
            xm, res = jnp.split(xr, 2, axis=-1)
            xc = jax.lax.conv_general_dilated(xm.swapaxes(1, 2), conv_w, (1,), [(D_CONV - 1, 0)], feature_group_count=D_INNER) + conv_b[:, None]
            xc = jax.nn.silu(xc.swapaxes(1, 2))
            y = _selective_scan(xc, A_log, D, x_proj_w, dt_proj_w, dt_proj_b)
            y = y * jax.nn.silu(res)
            return y @ out_proj_w.T

        def _moe(x, gate_w, w1, w2):
            gates = jax.nn.softmax(x @ gate_w.T, axis=-1)
            vals, idx = jax.lax.top_k(gates, K)
            vals = vals / jnp.sum(vals, axis=-1, keepdims=True)
            sparse = jnp.sum(jax.nn.one_hot(idx, E, dtype=x.dtype) * vals[..., None], axis=-2)
            h = jax.nn.gelu(jnp.einsum('bld,ehd->bleh', x, w1), approximate=False)
            y = jnp.einsum('bleh,edh->bled', h, w2)
            return jnp.einsum('bled,ble->bld', y, sparse)
        skip = x
        xn = _rmsnorm(x)
        xm = _mamba(xn, in_proj_w, conv_w, conv_b, x_proj_w, dt_proj_w, dt_proj_b, A_log, D, out_proj_w) + xn
        xm = _rmsnorm(xm)
        return _moe(xm, gate_w, w1, w2) + skip

    def _L0_xattn_ref(x, cross_input, Wk, bk, Wq, bq, Wv, bv, Wck, bck, Wcq, bcq, Wcv, bcv, Wp, bp):
        import jax, jax.numpy as jnp
        import numpy as np
        B, T, TC, C, CC, H = (2, 256, 64, 128, 64, 16)
        D = C // H

        def _heads(t):
            b, l, _ = t.shape
            return t.reshape(b, l, H, D).transpose(0, 2, 1, 3)
        scale = np.float32(1.0 / np.sqrt(D))
        q = _heads(x @ Wq + bq)
        k = _heads(x @ Wk + bk)
        v = _heads(x @ Wv + bv)
        att = jnp.einsum('bhqd,bhkd->bhqk', q, k) * scale
        causal = jnp.tril(jnp.ones((T, T), bool))
        att = jnp.where(causal[None, None], att, -jnp.inf)
        y = jnp.einsum('bhqk,bhkd->bhqd', jax.nn.softmax(att, axis=-1), v)
        qc = _heads(x @ Wcq + bcq)
        kc = _heads(cross_input @ Wck + bck)
        vc = _heads(cross_input @ Wcv + bcv)
        attc = jnp.einsum('bhqd,bhkd->bhqk', qc, kc) * scale
        y = y + jnp.einsum('bhqk,bhkd->bhqd', jax.nn.softmax(attc, axis=-1), vc)
        y = y.transpose(0, 2, 1, 3).reshape(x.shape[0], T, C)
        return y @ Wp + bp

    def _L0_ffn_ref(x, clip_x, clip_down, w_gate, w_up, w_down):
        import jax, jax.numpy as jnp
        import numpy as np
        QMAX = 127.0

        def _ste_round(v):
            return v + jax.lax.stop_gradient(jnp.round(v) - v)

        def _act_fake_quant(x, clip_factor):
            scale = jax.nn.sigmoid(clip_factor) * jnp.max(jnp.abs(x)) / QMAX
            return jnp.clip(_ste_round(x / scale), -QMAX - 1.0, QMAX) * scale

        def _weight_fake_quant(w):
            scale = jnp.max(jnp.abs(w), axis=1, keepdims=True) / QMAX
            return jnp.clip(_ste_round(w / scale), -QMAX - 1.0, QMAX) * scale
        xq = _act_fake_quant(x, clip_x[0])
        gate = jnp.einsum('bsh,ih->bsi', xq, _weight_fake_quant(w_gate))
        up = jnp.einsum('bsh,ih->bsi', xq, _weight_fake_quant(w_up))
        h = _act_fake_quant(jax.nn.silu(gate) * up, clip_down[0])
        return jnp.einsum('bsi,hi->bsh', h, _weight_fake_quant(w_down))

    def _L1_attn_ref(x, w_in, w_out, w_gate, b_gate, log_decay, frequency, coupling, w_mlp1, b_mlp1, w_mlp2, b_mlp2, ln1_g, ln1_b, ln2_g, ln2_b):
        import jax, jax.numpy as jnp
        import numpy as np
        import math
        B, T, D = (4, 512, 128)
        K, H, KH, C = (64, 4, 16, 64)
        MLP = 512
        EPS = 1e-05

        def _layernorm(x, g, b):
            m = jnp.mean(x, axis=-1, keepdims=True)
            v = jnp.mean((x - m) ** 2, axis=-1, keepdims=True)
            return (x - m) / jnp.sqrt(v + EPS) * g + b

        def _chunked_eigenstate(log_decay, frequency, beta_r, beta_i):
            Bt, Tt, Kt = beta_r.shape
            T_pad = (Tt + C - 1) // C * C
            if T_pad > Tt:
                beta_r = jnp.pad(beta_r, ((0, 0), (0, T_pad - Tt), (0, 0)))
                beta_i = jnp.pad(beta_i, ((0, 0), (0, T_pad - Tt), (0, 0)))
            n_chunks = T_pad // C
            mag = jax.nn.sigmoid(log_decay)
            powers = jnp.arange(C, dtype=log_decay.dtype)
            mag_pow = mag[:, None] ** powers[None, :]
            phases = frequency[:, None] * powers[None, :]
            kr = mag_pow * jnp.cos(phases)
            ki = mag_pow * jnp.sin(phases)
            ii = jnp.arange(C)
            idx = ii[None, :] - ii[:, None]
            mask = (idx >= 0).astype(kr.dtype)
            idxc = jnp.clip(idx, 0, C - 1)
            L_r = kr[:, idxc] * mask[None]
            L_i = ki[:, idxc] * mask[None]
            br = beta_r.reshape(Bt, n_chunks, C, Kt)
            bi = beta_i.reshape(Bt, n_chunks, C, Kt)
            intra_r = jnp.einsum('kjs,bnsk->bnjk', L_r, br) - jnp.einsum('kjs,bnsk->bnjk', L_i, bi)
            intra_i = jnp.einsum('kjs,bnsk->bnjk', L_r, bi) + jnp.einsum('kjs,bnsk->bnjk', L_i, br)
            first_col_r = L_r[:, :, 0]
            first_col_i = L_i[:, :, 0]

            def step(carry, intra):
                sr, si = carry
                ir, im = intra
                cr = first_col_r[None] * sr[:, :, None] - first_col_i[None] * si[:, :, None]
                ci = first_col_r[None] * si[:, :, None] + first_col_i[None] * sr[:, :, None]
                o_r = ir + jnp.transpose(cr, (0, 2, 1))
                o_i = im + jnp.transpose(ci, (0, 2, 1))
                return ((o_r[:, -1, :], o_i[:, -1, :]), (o_r, o_i))
            xs = (jnp.transpose(intra_r, (1, 0, 2, 3)), jnp.transpose(intra_i, (1, 0, 2, 3)))
            init = (jnp.zeros((Bt, Kt), beta_r.dtype), jnp.zeros((Bt, Kt), beta_r.dtype))
            _, (out_r, out_i) = jax.lax.scan(step, init, xs)
            c_r = jnp.transpose(out_r, (1, 0, 2, 3)).reshape(Bt, T_pad, Kt)[:, :Tt]
            c_i = jnp.transpose(out_i, (1, 0, 2, 3)).reshape(Bt, T_pad, Kt)[:, :Tt]
            return (c_r, c_i)
        residual = x
        x_norm = _layernorm(x, ln1_g, ln1_b)
        beta = x_norm @ w_in.T
        beta_r, beta_i = jnp.split(beta, 2, axis=-1)
        c_r, c_i = _chunked_eigenstate(log_decay, frequency, beta_r, beta_i)
        c_rh = c_r.reshape(x.shape[0], x.shape[1], H, KH)
        c_ih = c_i.reshape(x.shape[0], x.shape[1], H, KH)
        c_r = jnp.einsum('hjk,bthk->bthj', coupling, c_rh).reshape(x.shape[0], x.shape[1], K)
        c_i = jnp.einsum('hjk,bthk->bthj', coupling, c_ih).reshape(x.shape[0], x.shape[1], K)
        h = jnp.concatenate([c_r, c_i], axis=-1) @ w_out.T
        gate = jax.nn.sigmoid(x_norm @ w_gate.T + b_gate)
        x1 = residual + gate * h
        x2n = _layernorm(x1, ln2_g, ln2_b)
        mlp = jax.nn.silu(x2n @ w_mlp1.T + b_mlp1) @ w_mlp2.T + b_mlp2
        return x1 + mlp

    def _L1_xattn_ref(xx, ee, ln1_g, ln1_b, ln2_g, ln2_b, a1_wq, a1_wk, a1_wv, a1_li1_w, a1_li1_b, a1_lnx_g, a1_lnx_b, a1_lny_g, a1_lny_b, a1_ln3_g, a1_ln3_b, a1_li2_w, a1_li2_b, a1_li3_w, a1_li3_b, a2_wq, a2_wk, a2_wv, a2_li1_w, a2_li1_b, a2_lnx_g, a2_lnx_b, a2_lny_g, a2_lny_b, a2_ln3_g, a2_ln3_b, a2_li2_w, a2_li2_b, a2_li3_w, a2_li3_b, training):
        import jax, jax.numpy as jnp
        import numpy as np
        H, D, C1, C2, S, M, B, W = (16, 32, 128, 64, 256, 64, 2, 4)

        def _ln(x, g, b):
            m = jnp.mean(x, -1, keepdims=True)
            v = jnp.var(x, -1, keepdims=True)
            return (x - m) * jax.lax.rsqrt(v + 1e-05) * g + b

        def _mha(x, y, wq, wk, wv, li1_w, li1_b, lnx_g, lnx_b, lny_g, lny_b, ln3_g, ln3_b, li2_w, li2_b, li3_w, li3_b, causal):
            xn = _ln(x, lnx_g, lnx_b)
            yn = _ln(y, lny_g, lny_b)
            q = jnp.einsum('bsc,hcd->bhsd', xn, wq)
            k = jnp.einsum('btc,hcd->bhtd', yn, wk)
            v = jnp.einsum('btc,hcd->bhtd', yn, wv)
            a = jax.nn.softmax(jnp.einsum('bhsd,bhtd->bhst', q, k) * D ** (-0.5), axis=-1)
            if causal:
                s, t = (a.shape[-2], a.shape[-1])
                mask = (jnp.arange(t)[None, :] > jnp.arange(s)[:, None]).astype(a.dtype)
                a = a * mask
            o = jnp.einsum('bhst,bhtd->bhsd', a, v)
            o = o.transpose(0, 2, 1, 3).reshape(x.shape[0], x.shape[1], H * D)
            x_out = x + o @ li1_w + li1_b
            h = jax.nn.gelu(_ln(x_out, ln3_g, ln3_b) @ li2_w + li2_b, approximate=False)
            return x_out + h @ li3_w + li3_b
        x = _ln(xx, ln1_g, ln1_b)
        x = x + _mha(x, x, a1_wq, a1_wk, a1_wv, a1_li1_w, a1_li1_b, a1_lnx_g, a1_lnx_b, a1_lny_g, a1_lny_b, a1_ln3_g, a1_ln3_b, a1_li2_w, a1_li2_b, a1_li3_w, a1_li3_b, causal=True)
        x = _ln(x, ln2_g, ln2_b)
        return x + _mha(x, ee, a2_wq, a2_wk, a2_wv, a2_li1_w, a2_li1_b, a2_lnx_g, a2_lnx_b, a2_lny_g, a2_lny_b, a2_ln3_g, a2_ln3_b, a2_li2_w, a2_li2_b, a2_li3_w, a2_li3_b, causal=False)

    def _L1_ffn_ref(x, Wr, W1, W2):
        import jax, jax.numpy as jnp
        import numpy as np
        B, T, C = (4, 256, 128)
        E, F, K = (8, 256, 2)
        Bb, Tt, Cc = x.shape
        flat = x.reshape(-1, Cc)
        N = flat.shape[0]
        logits = flat @ Wr.T
        weights, ids = jax.lax.top_k(logits, K)
        weights = jax.nn.softmax(weights, axis=-1)
        rows = jnp.arange(N)[:, None]
        router_weights = jnp.zeros((N, E), dtype=flat.dtype).at[rows, ids].add(weights)
        h = jnp.einsum('nc,efc->nef', flat, W1)
        val, gate = (h[..., :F], h[..., F:])
        act = val * jax.nn.silu(gate)
        expert_outputs = jnp.einsum('nef,ecf->nec', act, W2)
        out = jnp.einsum('nec,ne->nc', expert_outputs, router_weights)
        return out.reshape(Bb, Tt, Cc)
    x = x + _L0_attn_ref(_layernorm(x, axis=-1), L0_attn_in_proj_w, L0_attn_conv_w, L0_attn_conv_b, L0_attn_x_proj_w, L0_attn_dt_proj_w, L0_attn_dt_proj_b, L0_attn_A_log, L0_attn_D, L0_attn_out_proj_w, L0_attn_gate_w, L0_attn_w1, L0_attn_w2)
    x = x + _L0_xattn_ref(_layernorm(x, axis=-1), ctx_512, L0_xattn_Wk, L0_xattn_bk, L0_xattn_Wq, L0_xattn_bq, L0_xattn_Wv, L0_xattn_bv, L0_xattn_Wck, L0_xattn_bck, L0_xattn_Wcq, L0_xattn_bcq, L0_xattn_Wcv, L0_xattn_bcv, L0_xattn_Wp, L0_xattn_bp)
    x = x + _L0_ffn_ref(_layernorm(x, axis=-1), L0_ffn_clip_x, L0_ffn_clip_down, L0_ffn_w_gate, L0_ffn_w_up, L0_ffn_w_down)
    x = x + _L1_attn_ref(_layernorm(x, axis=-1), L1_attn_w_in, L1_attn_w_out, L1_attn_w_gate, L1_attn_b_gate, L1_attn_log_decay, L1_attn_frequency, L1_attn_coupling, L1_attn_w_mlp1, L1_attn_b_mlp1, L1_attn_w_mlp2, L1_attn_b_mlp2, L1_attn_ln1_g, L1_attn_ln1_b, L1_attn_ln2_g, L1_attn_ln2_b)
    x = x + _L1_xattn_ref(_layernorm(x, axis=-1), ctx_512, L1_xattn_ln1_g, L1_xattn_ln1_b, L1_xattn_ln2_g, L1_xattn_ln2_b, L1_xattn_a1_wq, L1_xattn_a1_wk, L1_xattn_a1_wv, L1_xattn_a1_li1_w, L1_xattn_a1_li1_b, L1_xattn_a1_lnx_g, L1_xattn_a1_lnx_b, L1_xattn_a1_lny_g, L1_xattn_a1_lny_b, L1_xattn_a1_ln3_g, L1_xattn_a1_ln3_b, L1_xattn_a1_li2_w, L1_xattn_a1_li2_b, L1_xattn_a1_li3_w, L1_xattn_a1_li3_b, L1_xattn_a2_wq, L1_xattn_a2_wk, L1_xattn_a2_wv, L1_xattn_a2_li1_w, L1_xattn_a2_li1_b, L1_xattn_a2_lnx_g, L1_xattn_a2_lnx_b, L1_xattn_a2_lny_g, L1_xattn_a2_lny_b, L1_xattn_a2_ln3_g, L1_xattn_a2_ln3_b, L1_xattn_a2_li2_w, L1_xattn_a2_li2_b, L1_xattn_a2_li3_w, L1_xattn_a2_li3_b, 0)
    x = x + _L1_ffn_ref(_layernorm(x, axis=-1), L1_ffn_Wr, L1_ffn_W1, L1_ffn_W2)
    return x

_drawn_inputs = setup_inputs


def setup_inputs(seed=0):
    import zlib

    import numpy as np

    out = dict(_drawn_inputs(seed))
    spreads = {'L0_attn_conv_b': (0.0, 0.8),
     'L0_attn_D': (1.0, 0.6),
     'L0_xattn_bk': (0.0, 2.0),
     'L0_xattn_bq': (0.0, 0.721),
     'L0_xattn_bv': (0.0, 0.1),
     'L0_xattn_bck': (0.0, 2.0),
     'L0_xattn_bcq': (0.0, 0.608),
     'L0_xattn_bcv': (0.0, 0.1),
     'L0_xattn_bp': (0.0, 0.1),
     'L1_attn_b_gate': (-2.0, 0.6),
     'L1_attn_b_mlp1': (0.0, 0.377),
     'L1_attn_b_mlp2': (0.0, 0.288),
     'L1_attn_ln1_g': (1.0, 0.6),
     'L1_attn_ln1_b': (0.0, 0.645),
     'L1_attn_ln2_g': (1.0, 0.6),
     'L1_attn_ln2_b': (0.0, 0.335),
     'L1_xattn_ln1_g': (1.0, 0.2),
     'L1_xattn_ln1_b': (0.0, 0.1),
     'L1_xattn_ln2_g': (1.0, 0.2),
     'L1_xattn_ln2_b': (0.0, 0.1),
     'L1_xattn_a1_li1_b': (0.0, 0.4),
     'L1_xattn_a1_lnx_g': (1.0, 0.6),
     'L1_xattn_a1_lnx_b': (0.0, 0.8),
     'L1_xattn_a1_lny_g': (1.0, 0.6),
     'L1_xattn_a1_lny_b': (0.0, 0.8),
     'L1_xattn_a1_ln3_g': (1.0, 0.6),
     'L1_xattn_a1_ln3_b': (0.0, 0.8),
     'L1_xattn_a1_li2_b': (0.0, 0.8),
     'L1_xattn_a1_li3_b': (0.0, 1.189),
     'L1_xattn_a2_li1_b': (0.0, 0.405),
     'L1_xattn_a2_lnx_g': (1.0, 0.6),
     'L1_xattn_a2_lnx_b': (0.0, 0.8),
     'L1_xattn_a2_lny_g': (1.0, 0.6),
     'L1_xattn_a2_lny_b': (0.0, 0.8),
     'L1_xattn_a2_ln3_g': (1.0, 0.6),
     'L1_xattn_a2_ln3_b': (0.0, 0.8),
     'L1_xattn_a2_li2_b': (0.0, 0.8),
     'L1_xattn_a2_li3_b': (0.0, 0.38)}
    factors = {'L0_attn_in_proj_w': 8.0,
     'L0_attn_conv_w': 8.0,
     'L0_attn_x_proj_w': 8.0,
     'L0_attn_dt_proj_w': 8.0,
     'L0_attn_dt_proj_b': 8.0,
     'L0_attn_A_log': 8.0,
     'L0_attn_out_proj_w': 8.0,
     'L0_attn_gate_w': 3.268,
     'L0_attn_w1': 2.906,
     'L0_attn_w2': 2.844,
     'L0_ffn_w_gate': 8.0,
     'L0_ffn_w_up': 8.0,
     'L0_ffn_w_down': 8.0,
     'L1_attn_log_decay': 200.0,
     'L1_xattn_a1_wq': 8.0,
     'L1_xattn_a1_wk': 8.0,
     'L1_xattn_a1_wv': 8.0,
     'L1_xattn_a1_li1_w': 8.0,
     'L1_xattn_a1_li2_w': 4.907,
     'L1_xattn_a1_li3_w': 4.516,
     'L1_xattn_a2_wq': 8.0,
     'L1_xattn_a2_wk': 8.0,
     'L1_xattn_a2_wv': 5.93,
     'L1_xattn_a2_li1_w': 6.146,
     'L1_xattn_a2_li2_w': 4.597,
     'L1_xattn_a2_li3_w': 4.316,
     'L1_attn_frequency': 46.208}
    for name, (base, spread) in spreads.items():
        noise = np.random.default_rng([zlib.crc32(name.encode()), seed]).standard_normal(out[name].shape)
        drawn = base * np.exp(spread * noise) if base else spread * noise
        out[name] = jnp.asarray(drawn.astype(out[name].dtype))
    for name, factor in factors.items():
        out[name] = (out[name] * factor).astype(out[name].dtype)
    return out
```

```python
import math
from contextlib import ExitStack

import concourse.bass as bass
from concourse import mybir

F32 = mybir.dt.float32
BF16 = mybir.dt.bfloat16
I32 = mybir.dt.int32
U32 = mybir.dt.uint32
ACT = mybir.ActivationFunctionType
ALU = mybir.AluOpType
AX_X = mybir.AxisListType.X

P = 128
NB, L = 16, 256
NT = NB * L // P
TB = L // P
C = 128
EPS = 1e-5


def wait(eng, sem, value):
    if isinstance(value, int) and value <= 0:
        return
    eng.wait_ge(sem, value)


def turns(eng, n, first=1, last=0):
    for t in range(min(first, n)):
        yield t
    if n - last > first:
        with eng.Fori(first, n - last) as t:
            yield t
    for t in range(max(first, n - last), n):
        yield t


class Steps:

    def __init__(self, eng, sem):
        self.eng, self.sem = eng, sem
        self.base, self.n = 0, 0
        self.turn, self.per_turn, self.origin, self.peeled = None, None, None, 0

    def begin(self, turn):
        if isinstance(turn, int):
            if self.origin is None:
                self.base += self.n
            else:
                assert self.n == self.per_turn or self.n == 0, (self.n, self.per_turn)
                self.base = self.origin + turn * self.per_turn if not isinstance(self.turn, int) else self.base + self.n
            self.peeled = turn + 1
        else:
            if self.origin is None:
                self.per_turn = self.n
                self.base += self.n
                self.origin = self.base - self.peeled * self.per_turn
            assert self.n == self.per_turn, (self.n, self.per_turn)
            self.base = self.origin + turn * self.per_turn
        self.turn, self.n = turn, 0

    def done(self, ins):
        self.n += 1
        ins.then_inc(self.sem, 1)

    def sync(self):
        self.eng.wait_ge(self.sem, self.base + self.n)

    def do(self, ins):
        self.done(ins)
        self.sync()

    def hold(self, cell):
        self.sync()
        self.done(self.eng.tensor_tensor(cell[:, 1:2], cell[:, 0:1], cell[:, 0:1], ALU.add))


class Scope:

    def __init__(self, nc, ctx, prefix):
        self.nc, self.ctx, self.prefix, self.sems = nc, ctx, prefix, []
        ctx.callback(self.end)

    def end(self):
        if self.sems:
            self.nc.clear_and_free_semaphores(self.sems)
            self.nc.all_engine_barrier()

    def sb(self, name, shape, dt=F32):
        return self.ctx.enter_context(self.nc.sbuf_tensor(self.prefix + name, shape, dt))

    def ps(self, name, shape, dt=F32):
        return self.ctx.enter_context(self.nc.psum_tensor(self.prefix + name, shape, dt))

    def sem(self, name):
        self.sems.append(self.nc.alloc_semaphore(name=self.prefix + name))
        return self.sems[-1]


def load_all(sp, sem, pairs):
    for dst, src in pairs:
        sp.dma_start(dst, src).then_inc(sem, 16)
    return 16 * len(pairs)


class Norm:

    def __init__(self, sc, tag, tiles):
        self.tiles = tiles
        self.stat = sc.sb(tag + "stat", [P, tiles, 8])
        self.rstd = sc.sb(tag + "rstd", [P, tiles, 1])
        self.power = sc.sb(tag + "power", [P, tiles, 1])
        self.var = sc.sb(tag + "var", [P, tiles, 1])
        self.cell = sc.sb(tag + "cell", [P, 2])
        self.var_ready = sc.sem(tag + "var_ready")
        self.rstd_ready = sc.sem(tag + "rstd_ready")
        self.power_ready = sc.sem(tag + "power_ready")

    def setup(self, pool):
        pool.memset(self.power[:], -0.5).then_inc(self.power_ready, 1)
        pool.memset(self.cell[:], 0.0).then_inc(self.power_ready, 1)
        pool.wait_ge(self.power_ready, 2)

    def root(self, nc, pool, turn):
        pool.wait_ge(self.var_ready, turn + 1)
        nc.gpsimd.tensor_tensor(self.rstd[:], self.var[:], self.power[:], ALU.pow).then_inc(self.rstd_ready, 1)

    def rows(self, nc, ve, st, turn, src, dst):
        if isinstance(turn, int) and turn == 0:
            ve.wait_ge(self.power_ready, 2)
        st.hold(self.cell)
        for t in range(self.tiles):
            st.done(nc.vector.bn_stats(self.stat[:, t, 0:6], src(t)))
        st.hold(self.cell)
        for t in range(self.tiles):
            st.done(nc.vector.bn_aggr(self.stat[:, t, 6:8], self.stat[:, t, 0:6]))
        st.sync()
        nc.vector.tensor_scalar(self.var[:], self.stat[:, :, 7:8], EPS, None, ALU.add).then_inc(self.var_ready, 1)
        ve.wait_ge(self.rstd_ready, turn + 1)
        for t in range(self.tiles):
            st.done(nc.vector.tensor_scalar(dst(t), src(t), self.stat[:, t, 6:7], self.rstd[:, t, 0:1],
                                            ALU.subtract, ALU.mult))


def identity(nc, eng, ident, sem):
    eng.memset(ident, 0.0).then_inc(sem, 1)
    eng.wait_ge(sem, 1)
    eng.affine_select(out=ident, in_=ident, compare_op=ALU.not_equal, fill=1.0, base=0,
                      pattern=[[-1, ident.shape[-1]]], channel_multiplier=1).then_inc(sem, 1)


def mixture(nc, xres, ident, dram, tag, experts, chunks, glu, src=None):
    G = 4
    N = NT // G
    HK = chunks // 2 if glu else chunks
    E = experts
    with ExitStack() as ctx:
        sc = Scope(nc, ctx, tag)
        w1 = sc.sb("w1", [P, E, chunks, P])
        w2 = sc.sb("w2", [P, E, HK, C])
        wr = sc.sb("wr", [P, E])
        norm = Norm(sc, "n_", G) if src is None else None
        flag = sc.sb("flag", [P, 4])
        xn = sc.sb("xn", [P, G, C])
        xT = sc.sb("xT", [P, G * P])
        act = sc.sb("act", [P, 2, HK, G * P])
        silu = sc.sb("silu", [P, 2, G * P])
        col = sc.sb("col", [P, G, E])
        top = sc.sb("top", [P, G, 8])
        topi = sc.sb("topi", [P, G, 8], U32)
        topf = sc.sb("topf", [P, G, 2])
        pick = sc.sb("pick", [P, 2, G, E])
        low = sc.sb("low", [P, G, E])
        ex = sc.sb("ex", [P, G, E])
        tot = sc.sb("tot", [P, 2, G, 1])
        wgt = sc.sb("wgt", [P, G, E])
        hidP = [sc.ps(f"hidP{s}", [P, 2, G * P]) for s in range(2)]
        outP = [sc.ps(f"outP{s}", [P, G, C]) for s in range(2)]
        turnP = sc.ps("turnP", [P, G * P])
        gateP = sc.ps("gateP", [P, G, E])

        weights = sc.sem("weights")
        columns = sc.sem("columns")
        step = sc.sem("step")
        normed = sc.sem("normed")
        turned = sc.sem("turned")
        xT_ready = sc.sem("xT_ready")
        logits = sc.sem("logits")
        shifted = sc.sem("shifted")
        exped = sc.sem("exped")
        hidden = sc.sem("hidden")
        gated = sc.sem("gated")
        acted = sc.sem("acted")
        expert = sc.sem("expert")
        added = sc.sem("added")
        block = ctx.enter_context(nc.Block())

        @block.sync
        def _(sp):
            load_all(sp, weights, [(w1[:], dram[tag + "w1"]), (w2[:], dram[tag + "w2"]),
                                   (wr[:], dram[tag + "wr"])])

        @block.gpsimd
        def _(pool):
            pool.iota(col[:], pattern=[[0, G], [1, E]], base=0, channel_multiplier=0,
                      allow_small_or_imprecise_dtypes=True).then_inc(columns, 1)
            if norm:
                norm.setup(pool)
                for t in turns(pool, N):
                    norm.root(nc, pool, t)

        def tile(t, g):
            return (t * G + g)

        def rows(buf, t, g):
            i = t * G + g
            return buf[:, i, :] if isinstance(i, int) else buf[:, bass.ds(i, 1), :]

        @block.vector
        def _(ve):
            st = Steps(ve, step)
            st.do(nc.vector.memset(flag[:], 0.0))

            def front(t):
                wait(ve, turned, t)
                if src is None:
                    norm.rows(nc, ve, st, t, lambda g: rows(xres, t, g), lambda g: xn[:, g, :])
                else:
                    for g in range(G):
                        st.done(nc.vector.tensor_copy(xn[:, g, :], rows(src, t, g)))
                st.sync()
                nc.vector.tensor_copy(flag[:, 0:1], xn[:, 0, 0:1]).then_inc(normed, 1)

            def route(t):
                ve.wait_ge(logits, t + 1)
                st.hold(flag[:, 2:4])
                for g in range(G):
                    st.done(nc.vector.max(top[:, g, :], gateP[:, g, :]))
                st.sync()
                st.done(nc.vector.tensor_tensor(low[:], gateP[:], top[:, :, 0:1].to_broadcast([P, G, E]),
                                                ALU.subtract))
                st.sync()
                nc.vector.tensor_copy(flag[:, 1:2], low[:, 0, 0:1]).then_inc(shifted, 1)
                for g in range(G):
                    st.done(nc.vector.max_index(topi[:, g, :], top[:, g, :], gateP[:, g, :]))
                st.sync()
                st.do(nc.vector.tensor_copy(topf[:], topi[:, :, 0:2]))
                for k in range(2):
                    st.done(nc.vector.tensor_tensor(pick[:, k], col[:], topf[:, :, k:k + 1].to_broadcast([P, G, E]),
                                                    ALU.is_equal))
                st.sync()
                st.do(nc.vector.tensor_tensor(pick[:, 0], pick[:, 0], pick[:, 1], ALU.add))
                ve.wait_ge(exped, t + 1)
                st.do(nc.vector.tensor_tensor(ex[:], ex[:], pick[:, 0], ALU.mult))
                st.do(nc.vector.tensor_reduce(tot[:, 0], ex[:], AX_X, ALU.add))
                st.do(nc.vector.reciprocal(tot[:, 1], tot[:, 0]))
                st.do(nc.vector.tensor_tensor(wgt[:], ex[:], tot[:, 1].to_broadcast([P, G, E]), ALU.mult))

            def add(t, e):
                ve.wait_ge(expert, t * E + e + 1)
                wait(ve, added, t * E + e)
                for g in range(G):
                    ins = nc.vector.scalar_tensor_tensor(
                        out=rows(xres, t, g), in0=outP[e % 2][:, g, :].unsqueeze(1) if not isinstance(t, int) else outP[e % 2][:, g, :],
                        scalar=wgt[:, g, e:e + 1], in1=rows(xres, t, g), op0=ALU.mult, op1=ALU.add)
                ins.then_inc(added, 1)

            def glu_half(t, e, h):
                n = t * E * 2 + e * 2 + h
                ve.wait_ge(gated, n + 1)
                wait(ve, expert, t * E + e - 1)
                nc.vector.tensor_tensor(act[:, e % 2, h, :], hidP[h][:, 0, :], silu[:, h, :], ALU.mult).then_inc(acted, 1)

            ve.wait_ge(columns, 1)
            front(0)
            for t in turns(ve, N, last=1):
                st.begin(t)
                route(t)
                for e in range(E):
                    if glu:
                        for h in range(2):
                            glu_half(t, e, h)
                    if e > 0:
                        add(t, e - 1)
                    if e == E // 2 and not (isinstance(t, int) and t == N - 1):
                        front(t + 1)
                add(t, E - 1)

        @block.scalar
        def _(ac):
            def turn_in(t):
                ac.wait_ge(turned, t + 1)
                wait(ac, hidden, t * E * 2)
                nc.scalar.activation(xT[:], turnP[:], ACT.Copy).then_inc(xT_ready, 1)

            turn_in(0)
            for t in turns(ac, N, last=1):
                ac.wait_ge(shifted, t + 1)
                nc.scalar.activation(ex[:], low[:], ACT.Exp).then_inc(exped, 1)
                for e in range(E):
                    for h in range(2):
                        n = t * E * 2 + e * 2 + h
                        ac.wait_ge(hidden, n + 1)
                        if glu:
                            wait(ac, acted, n - 1)
                            nc.scalar.activation(silu[:, h, :], hidP[h][:, 1, :], ACT.Silu).then_inc(gated, 1)
                        else:
                            wait(ac, expert, t * E + e - 1)
                            nc.scalar.activation(act[:, e % 2, 2 * h:2 * h + 2, :], hidP[h][:], ACT.Gelu
                                                 ).then_inc(acted, 1)
                if not (isinstance(t, int) and t == N - 1):
                    turn_in(t + 1)

        @block.tensor
        def _(pe):
            pe.wait_ge(weights, 48)

            def front(t):
                pe.wait_ge(normed, t + 1)
                wait(pe, xT_ready, t)
                for g in range(G):
                    ins = nc.tensor.transpose(turnP[:, g * P:(g + 1) * P], xn[:, g, :], ident[:])
                ins.then_inc(turned, 1)

            def hid(t, e):
                for h in range(2):
                    wait(pe, acted, t * E * 2 + e * 2 + h - 1)
                    for c in range(2):
                        ins = nc.tensor.matmul(hidP[h][:, c, :], w1[:, e, 2 * h + c, :], xT[:], start=True, stop=True)
                    ins.then_inc(hidden, 1)

            def out(t, e):
                pe.wait_ge(acted, t * E * 2 + e * 2 + 2)
                wait(pe, added, t * E + e - 1)
                for g in range(G):
                    for k in range(HK):
                        ins = nc.tensor.matmul(outP[e % 2][:, g, :], act[:, e % 2, k, g * P:(g + 1) * P],
                                               w2[:, e, k, :], start=(k == 0), stop=(k == HK - 1))
                ins.then_inc(expert, 1)

            front(0)
            for t in turns(pe, N, last=1):
                pe.wait_ge(xT_ready, t + 1)
                wait(pe, shifted, t)
                for g in range(G):
                    ins = nc.tensor.matmul(gateP[:, g, :], xT[:, g * P:(g + 1) * P], wr[:], start=True, stop=True)
                ins.then_inc(logits, 1)
                for e in range(E):
                    hid(t, e)
                    if e > 0:
                        out(t, e - 1)
                    if e == E // 2 and not (isinstance(t, int) and t == N - 1):
                        front(t + 1)
                out(t, E - 1)


def layout1(i, np):
    w1 = i["L0_attn_w1"].reshape(8, 4, P, C)
    inp, xp = i["L0_attn_in_proj_w"], i["L0_attn_x_proj_w"]
    return {
        "m1_w1": w1.transpose(3, 0, 1, 2),
        "m1_w2": i["L0_attn_w2"].reshape(8, C, 4, P).transpose(3, 0, 2, 1),
        "m1_wr": i["L0_attn_gate_w"].T,
        "s1_win": inp.T,
        "s1_conv": i["L0_attn_conv_w"].reshape(256, 4).T,
        "s1_convb": i["L0_attn_conv_b"].reshape(2, P).T,
        "s1_xp_bc": xp[8:40].T.reshape(2, P, 32).transpose(1, 0, 2),
        "s1_xp_dt": xp[0:8].T.reshape(2, P, 8).transpose(1, 0, 2),
        "s1_dt": i["L0_attn_dt_proj_w"].T,
        "s1_dtb": i["L0_attn_dt_proj_b"].reshape(2, P).T,
        "s1_alog": i["L0_attn_A_log"].reshape(2, P, 16).transpose(1, 0, 2),
        "s1_d": i["L0_attn_D"].reshape(2, P).T,
        "s1_out": i["L0_attn_out_proj_w"].T.reshape(2, P, C).transpose(1, 0, 2),
    }


def mamba(nc, xres, x2, ident, dram):
    NS, GN = 16, 4
    NG = NS // GN
    TAPS = 4
    with ExitStack() as ctx:
        sc = Scope(nc, ctx, "s1_")
        win = sc.sb("win", [P, 512])
        conv = sc.sb("conv", [P, TAPS, 256])
        wtap = sc.sb("wtap", [P, TAPS, 256])
        convb = sc.sb("convb", [P, 2])
        xp_bc = sc.sb("xp_bc", [P, 2, 32])
        xp_dt = sc.sb("xp_dt", [P, 2, 8])
        dtw = sc.sb("dtw", [8, 256])
        dtb = sc.sb("dtb", [P, 2])
        alog = sc.sb("alog", [P, 2, NS])
        aneg = sc.sb("aneg", [P, 2, NS])
        dskip = sc.sb("dskip", [P, 2])
        wout = sc.sb("wout", [P, 2, C])
        sel = sc.sb("sel", [96, 32, P], BF16)
        norm = Norm(sc, "n_", TB)
        cell = sc.sb("cell", [P, 2])
        h = sc.sb("h", [P, TB, C])
        xn = [sc.sb(f"xn{s}", [P, TB, C]) for s in range(2)]
        sq = sc.sb("sq", [P, TB, C])
        ss = sc.sb("ss", [P, TB])
        rr = sc.sb("rr", [P, TB])
        xnT = sc.sb("xnT", [P, TAPS - 1 + L])
        u = [sc.sb(f"u{s}", [P, 2, L]) for s in range(2)]
        sres = [sc.sb(f"sres{s}", [P, 2, L]) for s in range(2)]
        dtT = sc.sb("dtT", [8, L])
        bc = sc.sb("bc", [32, L])
        bcr = sc.sb("bcr", [32, L])
        bcm = sc.sb("bcm", [32, L], BF16)
        bc3 = [sc.sb(f"bc3{s}", [96, L], BF16) for s in range(2)]
        pos = sc.sb("pos", [P, 2, L])
        mag = sc.sb("mag", [P, 2, L])
        em = sc.sb("em", [P, 2, L])
        lost = sc.sb("lost", [P, 2, L])
        lg = sc.sb("lg", [P, 2, L])
        delta = sc.sb("delta", [P, 2, L])
        du = sc.sb("du", [P, 2, L])
        decay = [sc.sb(f"decay{c}", [P, NS, L]) for c in range(2)]
        state = [sc.sb(f"state{c}", [P, NS, L]) for c in range(2)]
        ysum = sc.sb("ysum", [P, 2, L])
        yT = sc.sb("yT", [P, 2, L])
        o = sc.sb("o", [P, TB, C])
        osq = sc.sb("osq", [P, TB, C])
        oss = sc.sb("oss", [P, TB])
        orr = sc.sb("orr", [P, TB])

        bcP = [sc.ps(f"bcP{s}", [P, GN, L]) for s in range(2)]
        endsP = sc.ps("endsP", [P, 2, L])
        xmP = sc.ps("xmP", [P, 2, L])
        resP = sc.ps("resP", [P, 2, L])
        dblP = sc.ps("dblP", [P, 2, L])
        turnP, outP = endsP[:, 0, :], endsP[:, 1, :].rearrange("p (g c) -> p g c", g=TB)

        names = ("weights", "zeroed", "selected", "setup", "step", "h_ready", "xn_ready", "ss_ready", "rr_ready", "turned",
                 "xnT_ready", "projected", "u_ready", "sres_ready", "dbl_ready", "dt_copied", "bc_copied",
                 "bc3_ready", "pool_step", "pre_ready", "mag_ready", "em_ready", "lg_ready", "pos_ready", "plus_ready",
                 "delta_ready", "du_ready", "decayed", "bc_ready", "bc_used", "scanned", "summed", "yT_ready",
                 "out_ready", "oss_ready", "orr_ready", "o_ready", "x2_ready")
        S = {n: sc.sem(n) for n in names}
        block = ctx.enter_context(nc.Block())

        def rows(buf, t):
            return buf[:, TB * t:TB * t + TB, :] if isinstance(t, int) else buf[:, bass.ds(t * TB, TB), :]

        def row(buf, t, g):
            i = t * TB + g
            return buf[:, i, :] if isinstance(i, int) else buf[:, bass.ds(i, 1), :]

        def batches(eng):
            for j in turns(eng, NB // 2, last=1):
                for s in range(2):
                    yield 2 * j + s, s, not (isinstance(j, int) and j == NB // 2 - 1 and s == 1)

        LOADED = 16 * 13

        @block.sync
        def _(sp):
            pairs = [(conv[:, k, :], dram["s1_conv"][k:k + 1, :].to_broadcast([P, 256])) for k in range(TAPS)]
            pairs += [(win[:], dram["s1_win"]), (convb[:], dram["s1_convb"]), (xp_bc[:], dram["s1_xp_bc"]),
                      (xp_dt[:], dram["s1_xp_dt"]), (dtw[:], dram["s1_dt"]), (dtb[:], dram["s1_dtb"]),
                      (alog[:], dram["s1_alog"]), (dskip[:], dram["s1_d"]), (wout[:], dram["s1_out"])]
            assert load_all(sp, S["weights"], pairs) == LOADED

        @block.gpsimd
        def _(pool):
            pool.memset(sel[:], 0.0).then_inc(S["zeroed"], 1)
            pool.memset(xnT[:, 0:TAPS - 1], 0.0).then_inc(S["zeroed"], 1)
            for c in range(2):
                pool.memset(decay[c][:, :, 0:1], 0.0).then_inc(S["zeroed"], 1)
            pool.wait_ge(S["zeroed"], 4)
            for q in range(3):
                pool.affine_select(out=sel[32 * q:32 * q + 32], in_=sel[32 * q:32 * q + 32],
                                   compare_op=ALU.not_equal, fill=1.0, base=0, pattern=[[-1, 32], [0, P]],
                                   channel_multiplier=1).then_inc(S["selected"], 1)
                pool.wait_ge(S["selected"], q + 1)
            norm.setup(pool)
            st = Steps(pool, S["pool_step"])
            st.begin(0)
            st.do(nc.gpsimd.memset(cell[:], 0.0))
            spare = cell[0:1, :]

            def front(t, s):
                norm.root(nc, pool, t)
                pool.wait_ge(S["ss_ready"], t + 1)
                st.done(nc.gpsimd.tensor_tensor(rr[:], ss[:], norm.power[:, :, 0], ALU.pow))
                st.hold(spare)
                nc.gpsimd.tensor_scalar(rr[:], rr[:], 1e12, math.sqrt(C), ALU.min, ALU.mult).then_inc(S["rr_ready"], 1)
                pool.wait_ge(S["bc_copied"], t + 1)
                wait(pool, S["bc_ready"], (t - 1) * 2 * NG)
                st.hold(spare)
                st.do(nc.gpsimd.tensor_copy(bc3[s][0:32, :], bc[:]))
                st.done(nc.gpsimd.tensor_tensor(bcr[:], bc[:], bc3[s][0:32, :], ALU.subtract))
                st.hold(spare)
                st.done(nc.gpsimd.tensor_copy(bc3[s][32:64, :], bcr[:]))
                st.hold(spare)
                st.do(nc.gpsimd.tensor_copy(bcm[:], bcr[:]))
                nc.gpsimd.tensor_tensor(bc3[s][64:96, :], bcr[:], bcm[:], ALU.subtract).then_inc(S["bc3_ready"], 1)
                pool.wait_ge(S["bc3_ready"], t + 1)
                st.hold(spare)

            def lost_part(t):
                pool.wait_ge(S["em_ready"], t + 1)
                pool.wait_ge(S["plus_ready"], t + 1)
                st.hold(spare)
                st.do(nc.gpsimd.tensor_scalar(lost[:], em[:], 1.0, -1.0, ALU.add, ALU.add))
                st.do(nc.gpsimd.tensor_tensor(lost[:], em[:], lost[:], ALU.subtract))
                nc.gpsimd.tensor_tensor(pos[:], pos[:], lost[:], ALU.add).then_inc(S["pos_ready"], 1)

            def sums(t, g):
                pool.wait_ge(S["bc_used"], t * 2 * NG + NG + g + 1)
                if g == 0:
                    wait(pool, S["yT_ready"], t)
                n = GN * g
                for c in range(2):
                    st.done(nc.gpsimd.tensor_tensor(state[c][:, n:n + 2, :], state[c][:, n:n + 2, :],
                                                    state[c][:, n + 2:n + 4, :], ALU.add))
                st.sync()
                for c in range(2):
                    if g == 0:
                        ins = nc.gpsimd.tensor_tensor(ysum[:, c, :], state[c][:, n, :], state[c][:, n + 1, :], ALU.add)
                        if c == 0:
                            st.done(ins)
                        else:
                            ins.then_inc(S["summed"], 1)
                    else:
                        st.done(nc.gpsimd.tensor_tensor(state[c][:, n, :], state[c][:, n, :], state[c][:, n + 1, :], ALU.add))
                if g:
                    st.sync()
                    wait(pool, S["summed"], t * NG + g)
                    st.done(nc.gpsimd.tensor_tensor(ysum[:, 0, :], ysum[:, 0, :], state[0][:, n, :], ALU.add))
                    nc.gpsimd.tensor_tensor(ysum[:, 1, :], ysum[:, 1, :], state[1][:, n, :], ALU.add).then_inc(S["summed"], 1)
                    st.sync()

            def root_out(t):
                pool.wait_ge(S["oss_ready"], t + 1)
                st.done(nc.gpsimd.tensor_tensor(orr[:], oss[:], norm.power[:, :, 0], ALU.pow))
                st.hold(spare)
                nc.gpsimd.tensor_scalar(orr[:], orr[:], 1e12, math.sqrt(C), ALU.min, ALU.mult).then_inc(S["orr_ready"], 1)

            front(0, 0)
            lost_part(0)
            for t, s, more in batches(pool):
                st.begin(t)
                if not (isinstance(t, int) and t == 0):
                    root_out(t - 1)
                if more:
                    front(t + 1, 1 - s)
                for g in range(NG):
                    sums(t, g)
                    if g == 1 and more:
                        lost_part(t + 1)
            root_out(NB - 1)

        @block.scalar
        def _(ac):
            ac.wait_ge(S["weights"], LOADED)
            nc.scalar.activation(aneg[:], alog[:], ACT.Exp).then_inc(S["setup"], 1)

            def front(t, s):
                ac.wait_ge(S["turned"], t + 1)
                wait(ac, S["projected"], 2 * t)
                nc.scalar.activation(xnT[:, TAPS - 1:], turnP, ACT.Copy).then_inc(S["xnT_ready"], 1)
                ac.wait_ge(S["projected"], 2 * t + 1)
                wait(ac, S["yT_ready"], t - 1)
                for c in range(2):
                    ins = nc.scalar.activation(u[s][:, c, :], xmP[:, c, :], ACT.Silu, bias=convb[:, c:c + 1])
                ins.then_inc(S["u_ready"], 1)
                ac.wait_ge(S["projected"], 2 * t + 2)
                nc.scalar.activation(sres[s][:], resP[:], ACT.Silu).then_inc(S["sres_ready"], 1)
                ac.wait_ge(S["dbl_ready"], t + 1)
                nc.scalar.activation(dtT[:], dblP[0:8, 1, :], ACT.Copy).then_inc(S["dt_copied"], 1)
                wait(ac, S["bc3_ready"], t)
                nc.scalar.activation(bc[:], dblP[0:32, 0, :], ACT.Copy).then_inc(S["bc_copied"], 1)

            def soft(t):
                ac.wait_ge(S["plus_ready"], t + 1)
                for c in range(2):
                    ins = nc.scalar.activation(mag[:, c, :], xmP[:, c, :], ACT.Abs, bias=dtb[:, c:c + 1])
                ins.then_inc(S["mag_ready"], 1)
                ac.wait_ge(S["mag_ready"], t + 1)
                wait(ac, S["pos_ready"], t)
                nc.scalar.activation(em[:], mag[:], ACT.Exp, scale=-1.0).then_inc(S["em_ready"], 1)
                ac.wait_ge(S["em_ready"], t + 1)
                nc.scalar.activation(lg[:], em[:], ACT.Ln, bias=1.0).then_inc(S["lg_ready"], 1)

            def decays(t):
                ac.wait_ge(S["delta_ready"], t + 1)
                if isinstance(t, int) and t == 0:
                    ac.wait_ge(S["setup"], 2)
                    ac.wait_ge(S["zeroed"], 4)
                for c in range(2):
                    wait(ac, S["scanned"], 2 * t + c - 1)
                    for n in range(NS):
                        ins = nc.scalar.activation(decay[c][:, n, 1:], delta[:, c, 1:], ACT.Exp, scale=aneg[:, c, n:n + 1])
                    ins.then_inc(S["decayed"], 1)

            front(0, 0)
            soft(0)
            for t, s, more in batches(ac):
                decays(t)
                if more:
                    front(t + 1, 1 - s)
                    soft(t + 1)

        @block.tensor
        def _(pe):
            pe.wait_ge(S["weights"], LOADED)

            def spread(t, s, k):
                r = t * 2 * NG + k
                wait(pe, S["bc_used"], r - 1)
                if k == 0:
                    pe.wait_ge(S["bc3_ready"], t + 1)
                for n in range(GN):
                    ins = nc.tensor.matmul(bcP[k % 2][:, n, :], sel[:, GN * k + n, :], bc3[s][:], start=True, stop=True)
                ins.then_inc(S["bc_ready"], 1)

            def front(t, s):
                pe.wait_ge(S["xn_ready"], t + 1)
                wait(pe, S["xnT_ready"], t)
                for g in range(TB):
                    ins = nc.tensor.transpose(turnP[:, g * P:(g + 1) * P], xn[s][:, g, :], ident[:])
                ins.then_inc(S["turned"], 1)
                pe.wait_ge(S["xnT_ready"], t + 1)
                wait(pe, S["delta_ready"], t)
                for c in range(2):
                    for k in range(TAPS):
                        ins = nc.tensor.matmul(xmP[:, c, :], wtap[:, k, c * P:(c + 1) * P], xnT[:, k:k + L],
                                               start=(k == 0), stop=(k == TAPS - 1))
                ins.then_inc(S["projected"], 1)
                wait(pe, S["sres_ready"], t)
                for c in range(2):
                    ins = nc.tensor.matmul(resP[:, c, :], win[:, 256 + c * P:256 + (c + 1) * P], xnT[:, TAPS - 1:],
                                           start=True, stop=True)
                ins.then_inc(S["projected"], 1)
                pe.wait_ge(S["u_ready"], t + 1)
                wait(pe, S["bc_copied"], t)
                for w, m, j in ((xp_dt, 8, 1), (xp_bc, 32, 0)):
                    for c in range(2):
                        ins = nc.tensor.matmul(dblP[0:m, j, :], w[:, c, :], u[s][:, c, :], start=(c == 0), stop=(c == 1))
                ins.then_inc(S["dbl_ready"], 1)
                pe.wait_ge(S["dt_copied"], t + 1)
                for c in range(2):
                    ins = nc.tensor.matmul(xmP[:, c, :], dtw[:, c * P:(c + 1) * P], dtT[:], start=True, stop=True)
                ins.then_inc(S["pre_ready"], 1)

            def out(t):
                pe.wait_ge(S["yT_ready"], t + 1)
                wait(pe, S["o_ready"], t)
                for g in range(TB):
                    for c in range(2):
                        ins = nc.tensor.matmul(outP[:, g, :], yT[:, c, g * P:(g + 1) * P], wout[:, c, :],
                                               start=(c == 0), stop=(c == 1))
                ins.then_inc(S["out_ready"], 1)

            pe.wait_ge(S["setup"], 3)
            pe.wait_ge(S["selected"], 3)
            front(0, 0)
            for t, s, more in batches(pe):
                for k in range(NG):
                    spread(t, s, k)
                    if k == 0 and not (isinstance(t, int) and t == 0):
                        out(t - 1)
                if more:
                    front(t + 1, 1 - s)
                for k in range(NG, 2 * NG):
                    spread(t, s, k)
            out(NB - 1)

        @block.vector
        def _(ve):
            ve.wait_ge(S["setup"], 1)
            nc.vector.tensor_scalar(aneg[:], aneg[:], -1.0, None, ALU.mult).then_inc(S["setup"], 1)
            st = Steps(ve, S["step"])
            st.begin(0)
            for k in range(TAPS):
                ins = nc.vector.tensor_tensor(wtap[:, k, :], win[:, 0:256], conv[:, k, :], ALU.mult)
            ins.then_inc(S["setup"], 1)

            def front1(t):
                norm.rows(nc, ve, st, t, lambda g: row(xres, t, g), lambda g: h[:, g, :])
                st.sync()
                for g in range(TB):
                    ins = nc.vector.tensor_tensor_reduce(sq[:, g, :], h[:, g, :], h[:, g, :], 1.0, 0.0, ALU.mult,
                                                         ALU.add, ss[:, g:g + 1])
                    if g < TB - 1:
                        st.done(ins)
                ins.then_inc(S["ss_ready"], 1)
                ve.tensor_tensor(rows(xres, t), rows(xres, t), h[:], ALU.add)

            def front2(t, s):
                ve.wait_ge(S["rr_ready"], t + 1)
                wait(ve, S["turned"], t)
                for g in range(TB):
                    ins = nc.vector.tensor_scalar(xn[s][:, g, :], h[:, g, :], rr[:, g:g + 1], None, ALU.mult)
                ins.then_inc(S["xn_ready"], 1)

            def front3(t):
                ve.wait_ge(S["pre_ready"], t + 1)
                for c in range(2):
                    ins = nc.vector.tensor_scalar(pos[:, c, :], xmP[:, c, :], dtb[:, c:c + 1], 0.0, ALU.add, ALU.max)
                ins.then_inc(S["plus_ready"], 1)

            def front4(t, s):
                ve.wait_ge(S["lg_ready"], t + 1)
                ve.wait_ge(S["pos_ready"], t + 1)
                wait(ve, S["decayed"], 2 * t)
                nc.vector.tensor_tensor(delta[:], pos[:], lg[:], ALU.add).then_inc(S["delta_ready"], 1)
                ve.wait_ge(S["delta_ready"], t + 1)
                nc.vector.tensor_tensor(du[:], delta[:], u[s][:], ALU.mult).then_inc(S["du_ready"], 1)

            def inputs(t, g):
                r = t * 2 * NG + g
                ve.wait_ge(S["bc_ready"], r + 1)
                wait(ve, S["summed"], (t - 1) * NG + g + 1)
                if g == 0:
                    ve.wait_ge(S["du_ready"], t + 1)
                for c in range(2):
                    ins = nc.vector.tensor_tensor(state[c][:, GN * g:GN * g + GN, :], bcP[g % 2][:],
                                                  du[:, c:c + 1, :].to_broadcast([P, GN, L]), ALU.mult)
                    if c == 0:
                        st.done(ins)
                ins.then_inc(S["bc_used"], 1)

            def scan(t, c):
                ve.wait_ge(S["decayed"], 2 * t + c + 1)
                if c == 0:
                    ve.wait_ge(S["bc_used"], t * 2 * NG + NG)
                flat = lambda b: b[:].rearrange("p n l -> p (n l)")
                nc.vector.tensor_tensor_scan(flat(state[c]), flat(decay[c]), flat(state[c]), 0.0, ALU.mult, ALU.add
                                             ).then_inc(S["scanned"], 1)

            def outputs(t, g):
                ve.wait_ge(S["bc_ready"], t * 2 * NG + NG + g + 1)
                if g == 0:
                    ve.wait_ge(S["scanned"], 2 * t + 2)
                for c in range(2):
                    part = state[c][:, GN * g:GN * g + GN, :]
                    ins = nc.vector.tensor_tensor(part, part, bcP[g % 2][:], ALU.mult)
                    if c == 0:
                        st.done(ins)
                ins.then_inc(S["bc_used"], 1)

            def gate(t, s):
                ve.wait_ge(S["summed"], t * NG + NG)
                ve.wait_ge(S["sres_ready"], t + 1)
                wait(ve, S["out_ready"], t)
                for c in range(2):
                    st.done(nc.vector.scalar_tensor_tensor(out=yT[:, c, :], in0=u[s][:, c, :], scalar=dskip[:, c:c + 1],
                                                           in1=ysum[:, c, :], op0=ALU.mult, op1=ALU.add))
                st.sync()
                nc.vector.tensor_tensor(yT[:], yT[:], sres[s][:], ALU.mult).then_inc(S["yT_ready"], 1)

            def out1(t, s):
                ve.wait_ge(S["out_ready"], t + 1)
                nc.vector.tensor_tensor(o[:], outP, xn[s][:], ALU.add).then_inc(S["o_ready"], 1)
                ve.wait_ge(S["o_ready"], t + 1)
                for g in range(TB):
                    ins = nc.vector.tensor_tensor_reduce(osq[:, g, :], o[:, g, :], o[:, g, :], 1.0, 0.0, ALU.mult,
                                                         ALU.add, oss[:, g:g + 1])
                    if g < TB - 1:
                        st.done(ins)
                ins.then_inc(S["oss_ready"], 1)

            def out2(t):
                ve.wait_ge(S["orr_ready"], t + 1)
                for g in range(TB):
                    ins = nc.vector.tensor_scalar(row(x2, t, g), o[:, g, :], orr[:, g:g + 1], None, ALU.mult)
                ins.then_inc(S["x2_ready"], 1)

            front1(0)
            front2(0, 0)
            front3(0)
            front4(0, 0)
            for t, s, more in batches(ve):
                st.begin(t)
                first = isinstance(t, int) and t == 0
                inputs(t, 0)
                if not first:
                    out1(t - 1, 1 - s)
                inputs(t, 1)
                if more:
                    front1(t + 1)
                inputs(t, 2)
                if not first:
                    out2(t - 1)
                if more:
                    front2(t + 1, 1 - s)
                inputs(t, 3)
                scan(t, 0)
                scan(t, 1)
                outputs(t, 0)
                if more:
                    front3(t + 1)
                outputs(t, 1)
                outputs(t, 2)
                outputs(t, 3)
                if more:
                    front4(t + 1, 1 - s)
                gate(t, s)
            out1(NB - 1, 1)
            out2(NB - 1)


def stage1(nc, xres, ident, dram):
    with ExitStack() as ctx:
        x2 = Scope(nc, ctx, "").sb("x2", [P, NT, C])
        mamba(nc, xres, x2, ident, dram)
        mixture(nc, xres, ident, dram, "m1_", 8, 4, False, src=x2)




def normalise(nc, tag, src, hat, affine=None, add_to=None, dst=None, twice=False):
    G = 4
    NORMS = (2 if affine else 1) + twice
    N = NT // G
    with ExitStack() as ctx:
        sc = Scope(nc, ctx, tag)
        norm = Norm(sc, "n_", G)
        gain = sc.sb("gain", [P, 2, C])
        loaded = sc.sem("loaded")
        step = sc.sem("step")
        block = ctx.enter_context(nc.Block())

        def row(buf, t, g):
            i = t * G + g
            return buf[:, i, :] if isinstance(i, int) else buf[:, bass.ds(i, 1), :]

        def rows(buf, t):
            return buf[:, G * t:G * t + G, :] if isinstance(t, int) else buf[:, bass.ds(t * G, G), :]

        @block.sync
        def _(sp):
            if affine:
                load_all(sp, loaded, [(gain[:, i, :], a.to_broadcast([P, C])) for i, a in enumerate(affine)])

        @block.gpsimd
        def _(pool):
            norm.setup(pool)
            for t in turns(pool, N):
                for n in range(NORMS):
                    norm.root(nc, pool, NORMS * t + n)

        @block.vector
        def _(ve):
            st = Steps(ve, step)
            if affine:
                ve.wait_ge(loaded, 32)
            for t in turns(ve, N):
                st.begin(t)
                if affine:
                    wide = lambda i: gain[:, i, :].unsqueeze(1).to_broadcast([P, G, C])
                    norm.rows(nc, ve, st, NORMS * t, lambda g: row(src, t, g), lambda g: row(dst, t, g))
                    if twice:
                        norm.rows(nc, ve, st, NORMS * t + 1, lambda g: row(dst, t, g), lambda g: row(dst, t, g))
                    st.sync()
                    st.do(nc.vector.tensor_tensor(rows(dst, t), rows(dst, t), wide(0), ALU.mult))
                    st.do(nc.vector.tensor_tensor(rows(dst, t), rows(dst, t), wide(1), ALU.add))
                    if add_to is not None:
                        st.done(nc.vector.tensor_tensor(rows(add_to, t), rows(add_to, t), rows(dst, t), ALU.add))
                    norm.rows(nc, ve, st, NORMS * t + NORMS - 1, lambda g: row(dst, t, g), lambda g: row(hat, t, g))
                else:
                    norm.rows(nc, ve, st, t, lambda g: row(src, t, g), lambda g: row(hat, t, g))


def mlp(nc, xres, ident, dram, tag, src, dst):
    G = 4
    N = NT // G
    W = G * P
    H = 4
    with ExitStack() as ctx:
        sc = Scope(nc, ctx, tag)
        w1 = sc.sb("w1", [P, H, P])
        b1 = sc.sb("b1", [P, H])
        w2 = sc.sb("w2", [P, H, C])
        b2 = sc.sb("b2", [1, C])
        ln = sc.sb("ln", [P, 2])
        ones = sc.sb("ones", [1, P])
        norm = Norm(sc, "n_", G)
        xn = sc.sb("xn", [P, G, C])
        seen = sc.sb("seen", [P, 1])
        xT = sc.sb("xT", [P, W])
        act = sc.sb("act", [P, H, W])
        turnP = sc.ps("turnP", [P, W])
        outP = sc.ps("outP", [P, G, C])
        hidP = [sc.ps(f"hidP{s}", [P, W]) for s in range(4)]
        names = ("loaded", "ones_ready", "step", "xn_ready", "turned", "xT_ready", "hidden", "acted", "out", "out_used")
        S = {n: sc.sem(n) for n in names}
        block = ctx.enter_context(nc.Block())

        def row(buf, t, g):
            i = t * G + g
            return buf[:, i, :] if isinstance(i, int) else buf[:, bass.ds(i, 1), :]

        def rows(buf, t):
            return buf[:, G * t:G * t + G, :] if isinstance(t, int) else buf[:, bass.ds(t * G, G), :]

        @block.sync
        def _(sp):
            load_all(sp, S["loaded"], [(w1[:], dram[tag + "w1"]), (b1[:], dram[tag + "b1"]), (w2[:], dram[tag + "w2"]),
                                       (b2[:], dram[tag + "b2"]), (ln[:], dram[tag + "ln"])])

        @block.gpsimd
        def _(pool):
            pool.memset(ones[:], 1.0).then_inc(S["ones_ready"], 1)
            norm.setup(pool)
            for t in turns(pool, N):
                norm.root(nc, pool, t)

        def last(t):
            return isinstance(t, int) and t == N - 1

        @block.scalar
        def _(ac):
            def turn_in(t):
                ac.wait_ge(S["turned"], t + 1)
                wait(ac, S["hidden"], t * H)
                nc.scalar.activation(xT[:], turnP[:], ACT.Identity, scale=ln[:, 0:1], bias=ln[:, 1:2]
                                     ).then_inc(S["xT_ready"], 1)

            ac.wait_ge(S["loaded"], 80)
            turn_in(0)
            for t in turns(ac, N, last=1):
                for c in range(H):
                    ac.wait_ge(S["hidden"], t * H + c + 1)
                    if c == 0:
                        wait(ac, S["out"], t)
                    nc.scalar.activation(act[:, c, :], hidP[c][:], ACT.Gelu, bias=b1[:, c:c + 1]).then_inc(S["acted"], 1)
                if not last(t):
                    turn_in(t + 1)

        @block.tensor
        def _(pe):
            pe.wait_ge(S["loaded"], 80)
            pe.wait_ge(S["ones_ready"], 1)

            def front(t):
                pe.wait_ge(S["xn_ready"], t + 1)
                wait(pe, S["xT_ready"], t)
                for g in range(G):
                    ins = nc.tensor.transpose(turnP[:, g * P:(g + 1) * P], xn[:, g, :], ident[:])
                ins.then_inc(S["turned"], 1)

            front(0)
            for t in turns(pe, N, last=1):
                pe.wait_ge(S["xT_ready"], t + 1)
                for c in range(H):
                    wait(pe, S["acted"], (t - 1) * H + c + 1)
                    nc.tensor.matmul(hidP[c][:], w1[:, c, :], xT[:], start=True, stop=True).then_inc(S["hidden"], 1)
                if not last(t):
                    front(t + 1)
                wait(pe, S["out_used"], t)
                pe.wait_ge(S["acted"], t * H + H)
                for g in range(G):
                    nc.tensor.matmul(outP[:, g, :], ones[:], b2[:], start=True, stop=False)
                    for c in range(H):
                        ins = nc.tensor.matmul(outP[:, g, :], act[:, c, g * P:g * P + P], w2[:, c, :], start=False, stop=(c == H - 1))
                ins.then_inc(S["out"], 1)

        @block.vector
        def _(ve):
            st = Steps(ve, S["step"])

            def front(t):
                st.done(nc.vector.tensor_tensor(rows(dst, t), rows(dst, t), rows(src, t), ALU.add))
                wait(ve, S["turned"], t)
                norm.rows(nc, ve, st, t, lambda g: row(src, t, g), lambda g: xn[:, g, :])
                st.sync()
                nc.vector.tensor_copy(seen[:], xn[:, 0, 0:1]).then_inc(S["xn_ready"], 1)

            front(0)
            for t in turns(ve, N, last=1):
                st.begin(t)
                if not last(t):
                    front(t + 1)
                ve.wait_ge(S["out"], t + 1)
                nc.vector.tensor_tensor(rows(dst, t), rows(dst, t), outP[:], ALU.add).then_inc(S["out_used"], 1)


def attend(nc, xres, ident, dram, tag, hat, base, dst, kind, D, ln, bias, ctx_ln):
    cross = kind == "cross"
    HN = 16
    U = 4 if cross else HN
    KC = 64 if cross else P
    KEYS = 64
    SCALE = 1.0 / math.sqrt(D)
    OC = HN * D
    OT = OC // P
    CUT = 384 if kind == "causal" else 512
    NEG = -1e30
    with ExitStack() as ctx:
        sc = Scope(nc, ctx, tag)
        wq = sc.sb("wq", [P, 4, P])
        wk = sc.sb("wk", [KC, 4, P])
        wv = sc.sb("wv", [KC, OC])
        wo = sc.sb("wo", [P, OT, C])
        bo = sc.sb("bo", [1, C])
        bq = sc.sb("bq", [P, 4])
        bk = sc.sb("bk", [P, 4])
        bqs = sc.sb("bqs", [P, 4])
        bv = sc.sb("bv", [1, OC])
        lnw = sc.sb("lnw", [P, 4])
        ones = sc.sb("ones", [1, P])
        ident16 = sc.sb("ident16", [P, P], BF16)
        mask16 = sc.sb("mask16", [P, P], BF16)
        mask = sc.sb("mask", [P, 3, P])
        hs = [sc.sb(f"hs{s}", [P, TB, C]) for s in range(2)]
        cell = sc.sb("cell", [P, 2])
        xqT = sc.sb("xqT", [P, L])
        xkT = xqT if not ln else sc.sb("xkT", [P, L])
        q = [sc.sb(f"q{s}", [P, 4, L]) for s in range(2)]
        k = [sc.sb(f"k{s}", [P, 4, KEYS if cross else L]) for s in range(2)]
        v = [sc.sb(f"v{s}", [P, 1 if cross else TB, OC]) for s in range(2)]
        nmax = sc.sb("nmax", [P, 4, 8])
        sub = [sc.sb(f"sub{i}", [P, 512]) for i in range(2)] if cross else None
        prob = [sc.sb(f"prob{i}", [P, CUT]) for i in range(2)]
        probT = [sc.sb(f"probT{i}", [P, 4 if cross else 3, P]) for i in range(2)]
        den = [sc.sb(f"den{s}", [P, TB, HN]) for s in range(2)]
        rden = sc.sb("rden", [P, TB, HN])
        o = sc.sb("o", [P, TB, OC])
        oT = sc.sb("oT", [P, TB, OT, P])
        if cross:
            craw = sc.sb("craw", [P, 8, 64])
            chat = sc.sb("chat", [P, 8, 64])
            cnorm = Norm(sc, "cn_", 8)
            cln = sc.sb("cln", [64, 2])
            yT = sc.sb("yT", [64, NB * KEYS])
            y = [sc.sb(f"y{s}", [64, 2, KEYS]) for s in range(2)]
        scoreP = [sc.ps(f"scoreP{i}", [P, 512]) for i in range(2)]
        probP = [sc.ps(f"probP{i}", [P, 4, P]) for i in range(2)]
        oP = sc.ps("oP", [P, 2, 512])
        itemP = [sc.ps(f"itemP{i}", [P, 512]) for i in range(2)]
        names = ["loaded", "ones_ready", "masks", "bias_ready", "ident16_ready", "cstep", "step", "pool_step", "staged", "scores",
                 "maxed", "subbed", "exped", "turned", "probT_ready", "pv", "densed", "normed", "yT_mm", "yT_ready", "chat_ready", "y_ready"]
        items = ["T", "Q0", "Q1", "K0", "K1", "V0", "V1", "O0", "O1", "L"]
        S = {n: sc.sem(n) for n in names}
        made = {n: sc.sem("made_" + n) for n in items}
        used = {n: sc.sem("used_" + n) for n in items}
        SLOT = {"O0": 0, "O1": 1, "L": 0, "T": 1, "Q0": 0, "Q1": 1, "K0": 0, "K1": 1, "V0": 0, "V1": 1}
        block = ctx.enter_context(nc.Block())

        def rows(buf, t):
            return buf[:, TB * t:TB * t + TB, :] if isinstance(t, int) else buf[:, bass.ds(t * TB, TB), :]

        def batches(eng):
            for j in turns(eng, NB // 2, last=1):
                for s in range(2):
                    yield 2 * j + s, s

        def last(t):
            return isinstance(t, int) and t == NB - 1

        def earlier(t, s, u, d):
            if u >= d:
                return t, s, u - d
            return None if isinstance(t, int) and t == 0 else (t - 1, 1 - s, u - d + U)

        loads = [(wq[:], dram[tag + "wq"]), (wk[:], dram[tag + "wk"]), (wv[:], dram[tag + "wv"]), (wo[:], dram[tag + "wo"]),
                 (bo[:], dram[tag + "bo"])]
        if bias:
            loads += [(bq[:], dram[tag + "bq"]), (bk[:], dram[tag + "bk"]), (bv[:], dram[tag + "bv"])]
        if ln:
            loads += [(lnw[:], dram[tag + "ln"])]
        if cross:
            loads += [(craw[:], dram["ctx"])]
        if ctx_ln:
            loads += [(cln[:], dram[tag + "cln"])]
        LOADED = 16 * len(loads)
        if cross:
            WHEN = {0: [], 1: ["O0", "O1", "T"], 2: ["L", "Q0", "Q1"], 3: ["K0", "K1", "V0"]}
        else:
            WHEN = {3: ["O0"], 4: ["O1"], 5: ["L"], 6: ["T"], 8: ["Q0"], 9: ["Q1"], 10: ["K0"], 11: ["K1"], 12: ["V0"], 13: ["V1"]}
        FRONT = ["T", "Q0", "Q1", "K0", "K1", "V0"] + ([] if cross else ["V1"])
        BACK = ["O0", "O1", "L"]

        def extras(t, s, u, doing):
            for n in WHEN.get(u, []):
                if n in BACK:
                    if not (isinstance(t, int) and t == 0):
                        doing(n, t - 1, 1 - s)
                elif not last(t):
                    doing(n, t + 1, 1 - s)

        @block.sync
        def _(sp):
            load_all(sp, S["loaded"], loads)

        @block.gpsimd
        def _(pool):
            pool.memset(ones[:], 1.0).then_inc(S["ones_ready"], 1)
            if kind == "causal":
                pool.memset(mask16[:], 0.0).then_inc(S["masks"], 1)
                pool.wait_ge(S["masks"], 1)
                pool.affine_select(out=mask16[:], in_=mask16[:], compare_op=ALU.is_ge, fill=NEG, base=0,
                                   pattern=[[-1, P]], channel_multiplier=1).then_inc(S["masks"], 1)
            if kind == "after":
                pool.memset(mask[:], 1.0).then_inc(S["masks"], 1)
                pool.wait_ge(S["masks"], 1)
                pool.affine_select(out=mask[:, 0:2, :], in_=mask[:, 0:2, :], compare_op=ALU.is_gt, fill=0.0, base=0,
                                   pattern=[[0, 2], [-1, P]], channel_multiplier=1).then_inc(S["masks"], 1)
            st = Steps(pool, S["pool_step"])
            st.begin(0)
            st.done(nc.gpsimd.memset(cell[:], 0.0))
            if cross:
                cnorm.setup(pool)
                if ctx_ln:
                    cnorm.root(nc, pool, 0)

            def stage_in(t, s):
                wait(pool, used["T"], t - 1)
                st.hold(cell)
                nc.gpsimd.tensor_copy(hs[s][:], rows(hat, t)).then_inc(S["staged"], 1)

            stage_in(0, 0)
            for t, s in batches(pool):
                st.begin(t)
                if not last(t):
                    stage_in(t + 1, 1 - s)

        @block.scalar
        def _(ac):
            ac.wait_ge(S["loaded"], LOADED)
            if kind == "causal":
                nc.scalar.activation(ident16[:], ident[:], ACT.Copy).then_inc(S["ident16_ready"], 1)
            if bias:
                nc.scalar.activation(bqs[:], bq[:], ACT.Copy, scale=SCALE).then_inc(S["bias_ready"], 1)
                ac.wait_ge(S["bias_ready"], 1)
            if cross:
                for i in range(2):
                    ac.wait_ge(S["yT_mm"], i + 1)
                    kw = dict(scale=cln[:, 0:1], bias=cln[:, 1:2]) if ctx_ln else {}
                    nc.scalar.activation(yT[:, 512 * i:512 * i + 512], itemP[i][0:64, :], ACT.Identity, **kw
                                         ).then_inc(S["yT_ready"], 1)
                ac.wait_ge(S["yT_ready"], 2)

            def take(n, b, s):
                if n in ("L",):
                    return
                P_ = itemP[SLOT[n]]
                ac.wait_ge(made[n], b + 1)
                if n == "T":
                    wait(ac, made["V0" if cross else "V1"], b)
                    if cross:
                        src = yT[:, b * KEYS:b * KEYS + KEYS] if isinstance(b, int) else yT[:, bass.ds(b * KEYS, KEYS)]
                        nc.scalar.activation(y[s][:], src.unsqueeze(1).to_broadcast([64, 2, KEYS]), ACT.Copy).then_inc(S["y_ready"], 1)
                    if ln:
                        ins = nc.scalar.activation(xqT[:], P_[:, 0:L], ACT.Identity, scale=lnw[:, 0:1], bias=lnw[:, 1:2])
                        if not cross:
                            ins = nc.scalar.activation(xkT[:], P_[:, 0:L], ACT.Identity, scale=lnw[:, 2:3], bias=lnw[:, 3:4])
                    else:
                        ins = nc.scalar.activation(xqT[:], P_[:, 0:L], ACT.Copy)
                elif n in ("Q0", "Q1"):
                    wait(ac, S["scores"], (b - 1) * U)
                    i = 2 * int(n[1])
                    if bias:
                        for c in range(2):
                            ins = nc.scalar.activation(q[s][:, i + c, :], P_[:, c * L:c * L + L], ACT.Identity, scale=SCALE, bias=bqs[:, i + c:i + c + 1])
                    else:
                        ins = nc.scalar.activation(q[s][:, i:i + 2, :].rearrange("p c l -> p (c l)"), P_[:], ACT.Copy, scale=SCALE)
                elif n in ("K0", "K1"):
                    wait(ac, S["scores"], (b - 1) * U)
                    i = 2 * int(n[1])
                    w = KEYS if cross else L
                    if bias:
                        for c in range(2):
                            ins = nc.scalar.activation(k[s][:, i + c, :], P_[:, c * w:c * w + w], ACT.Identity, bias=bk[:, i + c:i + c + 1])
                    else:
                        ins = nc.scalar.activation(k[s][:, i:i + 2, :].rearrange("p c l -> p (c l)"), P_[:, 0:2 * w], ACT.Copy)
                elif n in ("V0", "V1"):
                    wait(ac, S["pv"], (b - 1) * U)
                    ins = nc.scalar.activation(v[s][:, int(n[1]), :], P_[:, 0:OC], ACT.Copy)
                else:
                    r = int(n[1])
                    wait(ac, made["L"], b)
                    ins = nc.scalar.activation(oT[:, r].rearrange("p c q -> p (c q)"), P_[:, 0:OC], ACT.Copy)
                ins.then_inc(used[n], 1)

            def exps(t, s, u):
                i = u % 2
                n = t * U + u
                wait(ac, S["turned"], n - 1)
                if cross:
                    ac.wait_ge(S["subbed"], n + 1)
                    wait(ac, S["densed"], n - 1)
                    nc.scalar.activation(prob[i][:], sub[i][:], ACT.Exp).then_inc(S["exped"], 1)
                else:
                    ac.wait_ge(S["maxed"], n + 1)
                    if u == 0:
                        wait(ac, S["normed"], t - 1)
                    cut = ((0, 128), (128, 384)) if kind == "causal" else ((0, 256), (256, 512))
                    for r, (a, b) in enumerate(cut):
                        ins = nc.scalar.activation(prob[i][:, a:b], scoreP[i][:, a:b], ACT.Exp, bias=nmax[:, u % 4, r:r + 1],
                                                   accum_out=den[s][:, r, u:u + 1])
                    ins.then_inc(S["exped"], 1)

            def turn_out(t, s, u):
                ac.wait_ge(S["turned"], t * U + u + 1)
                wait(ac, S["pv"], t * U + u - 1)
                nc.scalar.activation(probT[u % 2][:], probP[u % 2][:], ACT.Copy).then_inc(S["probT_ready"], 1)

            for n in FRONT:
                take(n, 0, 0)
            for t, s in batches(ac):
                for u in range(U):
                    exps(t, s, u)
                    if cross:
                        e = earlier(t, s, u, 1)
                        if e:
                            turn_out(*e)
                    extras(t, s, u, take)
            if cross:
                turn_out(NB - 1, 1, U - 1)
            for n in BACK:
                take(n, NB - 1, 1)

        @block.tensor
        def _(pe):
            pe.wait_ge(S["loaded"], LOADED)
            pe.wait_ge(S["ones_ready"], 1)
            if kind == "causal":
                pe.wait_ge(S["ident16_ready"], 1)
                pe.wait_ge(S["masks"], 2)
            if cross:
                if ctx_ln:
                    pe.wait_ge(S["chat_ready"], 1)
                for i in range(2):
                    for j in range(4):
                        ins = nc.tensor.transpose(itemP[i][0:64, j * P:j * P + P], (chat if ctx_ln else craw)[:, 4 * i + j, :], ident[:])
                    ins.then_inc(S["yT_mm"], 1)
                pe.wait_ge(S["yT_ready"], 2)

            def make(n, b, s):
                P_ = itemP[SLOT[n]]
                cap = lambda x: min(x, NB) if isinstance(x, int) else x
                vlast = "K1" if cross else "V1"
                pred = {"O0": [("V0", cap(b + 2))], "O1": [(vlast, cap(b + 2))], "L": [("O0", b + 1), ("O1", b + 1)],
                        "T": [("O1", b - 1), (vlast, b)], "Q0": [("L", b - 1), ("V0", b)],
                        "Q1": [("T", b + 1)], "K0": [("Q0", b + 1)], "K1": [("Q1", b + 1)], "V0": [("K0", b + 1)],
                        "V1": [("K1", b + 1)]}[n]
                for m, c in pred:
                    wait(pe, used[m], c)
                if n == "T":
                    pe.wait_ge(S["staged"], b + 1)
                    for g in range(TB):
                        ins = nc.tensor.transpose(P_[:, g * P:g * P + P], hs[s][:, g, :], ident[:])
                elif n in ("Q0", "Q1"):
                    pe.wait_ge(used["T"], b + 1)
                    for c in range(2):
                        ins = nc.tensor.matmul(P_[:, c * L:c * L + L], wq[:, 2 * int(n[1]) + c, :], xqT[:], start=True, stop=True)
                elif n in ("K0", "K1"):
                    w = KEYS if cross else L
                    if cross:
                        pe.wait_ge(S["y_ready"], b + 1)
                    for c in range(2):
                        ins = nc.tensor.matmul(P_[:, c * w:c * w + w], wk[:, 2 * int(n[1]) + c, :], y[s][:, 0, :] if cross else xkT[:],
                                               start=True, stop=True)
                elif n in ("V0", "V1"):
                    g = int(n[1])
                    keys = y[s][:].rearrange("p a k -> p (a k)") if cross else xkT[:, g * P:g * P + P]
                    if bias:
                        nc.tensor.matmul(P_[:, 0:OC], ones[:], bv[:], start=True, stop=False)
                    ins = nc.tensor.matmul(P_[:, 0:OC], keys, wv[:], start=not bias, stop=True)
                elif n in ("O0", "O1"):
                    pe.wait_ge(S["normed"], b + 1)
                    for c in range(OT):
                        ins = nc.tensor.transpose(P_[:, c * P:c * P + P], o[:, int(n[1]), c * P:c * P + P], ident[:])
                else:
                    for g in range(TB):
                        nc.tensor.matmul(P_[:, g * P:g * P + P], ones[:], bo[:], start=True, stop=False)
                        for c in range(OT):
                            ins = nc.tensor.matmul(P_[:, g * P:g * P + P], oT[:, g, c, :], wo[:, c, :], start=False, stop=(c == OT - 1))
                ins.then_inc(made[n], 1)

            def scores(t, s, u):
                i = u % 2
                n = t * U + u
                if u == 0:
                    pe.wait_ge(used["K1"], t + 1)
                    pe.wait_ge(used["Q1"], t + 1)
                wait(pe, S["subbed"] if cross else S["exped"], n - 1)
                if cross:
                    for r in range(TB):
                        for m in range(4):
                            at = (r * 4 + m) * 64
                            ins = nc.tensor.matmul(scoreP[i][:, at:at + 64], q[s][32 * u:32 * u + 32, m, r * P:r * P + P],
                                                   k[s][32 * u:32 * u + 32, m, :], start=True, stop=True)
                else:
                    j, c = u % 4, u // 4
                    qa = lambda r: q[s][32 * j:32 * j + 32, c, r * P:r * P + P]
                    ka = lambda a, b: k[s][32 * j:32 * j + 32, c, a:b]
                    if kind == "causal":
                        nc.tensor.matmul(scoreP[i][:, 0:128], qa(0), ka(0, 128), start=True, stop=False)
                        nc.tensor.matmul(scoreP[i][:, 0:128], ident16[:], mask16[:], start=False, stop=True)
                        nc.tensor.matmul(scoreP[i][:, 128:256], qa(1), ka(0, 128), start=True, stop=True)
                        nc.tensor.matmul(scoreP[i][:, 256:384], qa(1), ka(128, 256), start=True, stop=False)
                        ins = nc.tensor.matmul(scoreP[i][:, 256:384], ident16[:], mask16[:], start=False, stop=True)
                    else:
                        for r in range(TB):
                            ins = nc.tensor.matmul(scoreP[i][:, r * L:r * L + L], qa(r), ka(0, L), start=True, stop=True)
                ins.then_inc(S["scores"], 1)

            BLOCKS = {"causal": (0, 128, 256), "after": (0, 384, 128), "cross": (0, 128, 256, 384)}[kind]

            def turn(t, s, u):
                i = u % 2
                pe.wait_ge(S["exped"], t * U + u + 1)
                wait(pe, S["probT_ready"], t * U + u - 1)
                for m, a in enumerate(BLOCKS):
                    ins = nc.tensor.transpose(probP[i][:, m, :], prob[i][:, a:a + P], ident[:])
                ins.then_inc(S["turned"], 1)

            def pv(t, s, u):
                i = u % 2
                pe.wait_ge(S["probT_ready"], t * U + u + 1)
                if u == 0:
                    wait(pe, S["normed"], t)
                    pe.wait_ge(used["V0" if cross else "V1"], t + 1)
                if cross:
                    for r in range(TB):
                        for m in range(4):
                            h = 4 * m + u
                            b = 64 * (m % 2)
                            at = (8 * r + 4 * (m // 2) + u) * D
                            ins = nc.tensor.matmul(oP[:, m % 2, at:at + D], probT[i][b:b + 64, 2 * r + m // 2, :],
                                                   v[s][b:b + 64, 0, h * D:h * D + D], start=True, stop=True)
                else:
                    plan = {"causal": ((0, 0, 0), (1, 1, 0), (2, 1, 1)), "after": ((0, 0, 0), (2, 0, 1), (1, 1, 1))}[kind]
                    for n, (m, r, kt) in enumerate(plan):
                        first = n == 0 or plan[n - 1][1] != r
                        final = n == len(plan) - 1 or plan[n + 1][1] != r
                        ins = nc.tensor.matmul(oP[:, r, u * D:u * D + D], probT[i][:, m, :], v[s][:, kt, u * D:u * D + D],
                                               start=first, stop=final)
                ins.then_inc(S["pv"], 1)

            for n in FRONT:
                make(n, 0, 0)
            for t, s in batches(pe):
                for u in range(U):
                    scores(t, s, u)
                    for d, f in ((1, turn), (2, pv)):
                        e = earlier(t, s, u, d)
                        if e:
                            f(*e)
                    extras(t, s, u, make)
            turn(NB - 1, 1, U - 1)
            pv(NB - 1, 1, U - 2)
            pv(NB - 1, 1, U - 1)
            for n in BACK:
                make(n, NB - 1, 1)

        @block.vector
        def _(ve):
            st = Steps(ve, S["step"])
            st.begin(0)
            if cross:
                ve.wait_ge(S["loaded"], LOADED)
                if ctx_ln:
                    cst = Steps(ve, S["cstep"])
                    cst.begin(0)
                    cnorm.rows(nc, ve, cst, 0, lambda g: craw[:, g, :], lambda g: chat[:, g, :])
                    cst.sync()
                    nc.vector.tensor_copy(nmax[:, 0, 0:1], chat[:, 0, 0:1]).then_inc(S["chat_ready"], 1)
                    ve.wait_ge(S["chat_ready"], 1)
            if kind == "after":
                ve.wait_ge(S["masks"], 2)

            def maxes(t, s, u):
                n = t * U + u
                i = u % 2
                ve.wait_ge(S["scores"], n + 1)
                if cross:
                    wait(ve, S["exped"], n - 1)
                    if u == 0:
                        wait(ve, S["normed"], t - 1)
                    st.do(nc.vector.tensor_reduce(nmax[:, u % 4, :], scoreP[i][:].rearrange("p (a k) -> p a k", k=64), AX_X, ALU.max))
                    nc.vector.tensor_tensor(sub[i][:].rearrange("p (a k) -> p a k", k=64), scoreP[i][:].rearrange("p (a k) -> p a k", k=64),
                                            nmax[:, u % 4, :].unsqueeze(2).to_broadcast([P, 8, 64]), ALU.subtract).then_inc(S["subbed"], 1)
                else:
                    wait(ve, S["exped"], n - 3)
                    if kind == "causal":
                        for r, (a, b) in enumerate(((0, 128), (128, 384))):
                            ins = nc.vector.tensor_reduce(nmax[:, u % 4, r:r + 1], scoreP[i][:, a:b], AX_X, ALU.max, negate=True)
                    else:
                        ins = nc.vector.tensor_reduce(nmax[:, u % 4, 0:2], scoreP[i][:].rearrange("p (r k) -> p r k", r=2), AX_X, ALU.max, negate=True)
                    ins.then_inc(S["maxed"], 1)

            def turn_out(t, s, u):
                i = u % 2
                if cross:
                    ve.wait_ge(S["exped"], t * U + u + 1)
                    nc.vector.tensor_reduce(den[s][:].rearrange("p r (m u) -> p r m u", u=4)[:, :, :, u], prob[i][:].rearrange("p (r h k) -> p r h k", r=2, k=64),
                                            AX_X, ALU.add).then_inc(S["densed"], 1)
                    return
                ve.wait_ge(S["turned"], t * U + u + 1)
                wait(ve, S["pv"], t * U + u - 1)
                if kind == "causal":
                    nc.vector.tensor_copy(probT[i][:], probP[i][:, 0:3, :]).then_inc(S["probT_ready"], 1)
                else:
                    nc.vector.tensor_tensor(probT[i][:], probP[i][:, 0:3, :], mask[:], ALU.mult).then_inc(S["probT_ready"], 1)

            def norm_out(t, s):
                ve.wait_ge(S["pv"], t * U + U)
                wait(ve, made["O1"], t)
                if cross:
                    ve.wait_ge(S["densed"], t * U + U)
                st.do(nc.vector.reciprocal(rden[:], den[s][:]))
                if cross:
                    for r in range(TB):
                        for b in range(2):
                            ins = nc.vector.tensor_tensor(
                                o[:, r, :].rearrange("p (a b u d) -> p a b u d", a=2, b=2, d=D)[:, :, b],
                                oP[:, b, 8 * r * D:8 * r * D + 8 * D].rearrange("p (a u d) -> p a u d", a=2, d=D),
                                rden[:, r, :].rearrange("p (a b u) -> p a b u", a=2, b=2)[:, :, b].unsqueeze(3).to_broadcast([P, 2, 4, D]),
                                ALU.mult)
                            if (r, b) != (TB - 1, 1):
                                st.done(ins)
                    ins.then_inc(S["normed"], 1)
                    return
                for r in range(TB):
                    ins = nc.vector.tensor_tensor(o[:, r, :].rearrange("p (h d) -> p h d", d=D), oP[:, r, 0:OC].rearrange("p (h d) -> p h d", d=D),
                                                  rden[:, r, :].unsqueeze(2).to_broadcast([P, HN, D]), ALU.mult)
                    if r == 0:
                        st.done(ins)
                ins.then_inc(S["normed"], 1)

            def take(n, b, s):
                if n != "L":
                    return
                ve.wait_ge(made["L"], b + 1)
                nc.vector.tensor_tensor(rows(dst, b), rows(base, b), itemP[SLOT["L"]][:, 0:TB * P].rearrange("p (g c) -> p g c", g=TB),
                                        ALU.add).then_inc(used["L"], 1)

            for t, s in batches(ve):
                st.begin(t)
                for u in range(U):
                    maxes(t, s, u)
                    e = earlier(t, s, u, 1)
                    if e:
                        turn_out(*e)
                    if u == NORM_AT[cross] and not (isinstance(t, int) and t == 0):
                        norm_out(t - 1, 1 - s)
                    extras(t, s, u, take)
            turn_out(NB - 1, 1, U - 1)
            norm_out(NB - 1, 1)
            take("L", NB - 1, 1)


NORM_AT = {True: 1, False: 1}


def heads32(w, np):
    out = np.zeros((w.shape[0], 16, 32), w.dtype)
    out[:, :, 0:8] = w.reshape(w.shape[0], 16, 8)
    return out.reshape(w.shape[0], 4, P)


def layout2(i, np):
    g = lambda n: i["L0_xattn_" + n]
    laid = {"ctx": i["ctx_512"].reshape(8, P, 64).transpose(1, 0, 2)}
    for tag, c in (("s2s_", ""), ("s2c_", "c")):
        laid.update({tag + "wq": heads32(g("W" + c + "q"), np), tag + "wk": heads32(g("W" + c + "k"), np), tag + "wv": g("W" + c + "v"),
                     tag + "wo": g("Wp").reshape(P, 1, C),
                     tag + "bq": heads32(g("b" + c + "q").reshape(1, P), np)[0].T, tag + "bk": heads32(g("b" + c + "k").reshape(1, P), np)[0].T,
                     tag + "bv": g("b" + c + "v").reshape(1, P)})
    laid["s2s_bo"] = g("bp").reshape(1, C)
    laid["s2c_bo"] = np.zeros((1, C), np.float32)
    return laid


def stage2(nc, xres, ident, dram):
    with ExitStack() as ctx:
        hat = Scope(nc, ctx, "").sb("hat2", [P, NT, C])
        normalise(nc, "n2_", xres, hat)
        attend(nc, xres, ident, dram, "s2s_", hat, xres, xres, "causal", 8, False, True, False)
        attend(nc, xres, ident, dram, "s2c_", hat, xres, xres, "cross", 8, False, True, False)


def layout3(i, np):
    return {"s3_wg": i["L0_ffn_w_gate"], "s3_wu": i["L0_ffn_w_up"], "s3_wd": i["L0_ffn_w_down"],
            "s3_clip": np.concatenate([i["L0_ffn_clip_x"], i["L0_ffn_clip_down"]]).reshape(1, 2)}


def stage3(nc, xres, ident, dram):
    I = 352
    MC = [P, P, I - 2 * P]
    NC = len(MC)
    G = 4
    N = NT // G
    W = G * P
    QMAX = 127.0
    ROUND = 1.5 * 2.0 ** 23
    with ExitStack() as ctx:
        sc = Scope(nc, ctx, "s3_")
        wgu = sc.sb("wgu", [P, 2, NC, C])
        wd = sc.sb("wd", [P, I])
        clip = sc.sb("clip", [P, 2])
        sig = sc.sb("sig", [P, 2])
        wmax = sc.sb("wmax", [P, 2 * NC + 1])
        wscale = sc.sb("wscale", [P, 2 * NC + 1])
        winv = sc.sb("winv", [P, 2 * NC + 1])
        wguq = sc.sb("wguq", [P, 2, NC, C], BF16)
        wdq = sc.sb("wdq", [P, I], BF16)
        wguT = sc.sb("wguT", [P, 2, NC, P], BF16)
        wdT = sc.sb("wdT", [P, NC, C], BF16)
        ident16 = sc.sb("ident16", [P, P], BF16)
        ones = sc.sb("ones", [P, P])
        diag = sc.sb("diag", [P, P])
        wdrow = sc.sb("wdrow", [P, C])
        norm = Norm(sc, "n_", G)
        xn = sc.sb("xn", [P, NT, C])
        xq = sc.sb("xq", [P, 2 * G, C], BF16)
        xqT = sc.sb("xqT", [P, NT * P], BF16)
        xmax = sc.sb("xmax", [P, 1])
        xall = sc.sb("xall", [P, 1])
        scale = sc.sb("scale", [P, 2])
        inv = sc.sb("inv", [P, 2])
        guscale = sc.sb("guscale", [P, 2 * NC])
        hid = sc.sb("hid", [P, NC, NT * P])
        silu = sc.sb("silu", [P, NC, W])
        hmaxs = sc.sb("hmaxs", [P, N * NC])
        hmax = sc.sb("hmax", [P, 1])
        hall = sc.sb("hall", [P, 1])
        hq = [sc.sb(f"hq{s}", [P, NC, W], BF16) for s in range(2)]
        y = sc.sb("y", [P, W])
        gateP = sc.ps("gateP", [P, NC, W])
        upP = sc.ps("upP", [P, NC, W])
        turnP = [sc.ps(f"turnP{s}", [P, 2 * W], BF16) for s in range(2)]
        outP = [gateP[:, s, :] for s in range(2)]
        names = ("loaded", "filled", "flat", "step", "w_q", "w_turned", "wT", "sig_ready", "xmax_ready", "xall_ready",
                 "xq_ready", "turned", "xqT_ready", "diag_ready", "wdrow_turned", "wdrow_ready", "gate", "up", "silu_ready",
                 "hid_ready", "hmax_ready", "hall_ready", "hq_ready", "out", "out_used", "id16", "y_ready")
        S = {n: sc.sem(n) for n in names}
        block = ctx.enter_context(nc.Block())

        def pairs(eng):
            for j in turns(eng, N // 2):
                for s in range(2):
                    yield 2 * j + s, s

        def rows(buf, t, n=G):
            return buf[:, n * t:n * t + n, :] if isinstance(t, int) else buf[:, bass.ds(t * n, n), :]

        def row(buf, t, g):
            i = t * G + g
            return buf[:, i, :] if isinstance(i, int) else buf[:, bass.ds(i, 1), :]

        def cols(ap, t):
            return ap[..., t * W:t * W + W] if isinstance(t, int) else ap[..., bass.ds(t * W, W)]

        xqs = [xq[:, s * G:s * G + G, :] for s in range(2)]
        LOADS = 6

        @block.sync
        def _(sp):
            sp.wait_ge(S["filled"], 2)
            cut = lambda w: w[0:2 * P, :].rearrange("(c p) h -> p c h", p=P)
            load_all(sp, S["loaded"],
                     [(wgu[:, 0, 0:2, :], cut(dram["s3_wg"])), (wgu[:, 1, 0:2, :], cut(dram["s3_wu"])),
                      (wgu[0:MC[2], 0, 2, :], dram["s3_wg"][2 * P:I, :]),
                      (wgu[0:MC[2], 1, 2, :], dram["s3_wu"][2 * P:I, :]),
                      (wd[:], dram["s3_wd"]), (clip[:], dram["s3_clip"].to_broadcast([P, 2]))])

        @block.gpsimd
        def _(pool):
            pool.memset(wgu[:, :, 2, :], 1.0).then_inc(S["filled"], 1)
            pool.memset(ones[:], 1.0).then_inc(S["filled"], 1)
            norm.setup(pool)
            for t in turns(pool, N):
                norm.root(nc, pool, t)
            pool.wait_ge(S["xmax_ready"], 1)
            nc.gpsimd.partition_all_reduce(xall[:], xmax[:], P, bass.bass_isa.ReduceOp.max).then_inc(S["xall_ready"], 1)
            pool.wait_ge(S["hmax_ready"], 1)
            nc.gpsimd.partition_all_reduce(hall[:], hmax[:], P, bass.bass_isa.ReduceOp.max).then_inc(S["hall_ready"], 1)

        @block.scalar
        def _(ac):
            nc.scalar.activation(ident16[:], ident[:], ACT.Copy).then_inc(S["id16"], 1)
            ac.wait_ge(S["loaded"], 16 * LOADS)
            nc.scalar.activation(sig[:], clip[:], ACT.Sigmoid).then_inc(S["sig_ready"], 1)
            ac.wait_ge(S["w_turned"], 1)
            nc.scalar.activation(wguT[:].rearrange("p a c f -> p (a c f)"), turnP[0][:, 0:2 * NC * P], ACT.Copy
                                 ).then_inc(S["wT"], 1)
            ac.wait_ge(S["w_turned"], 2)
            for c in range(NC):
                ins = nc.scalar.activation(wdT[0:MC[c], c, :], turnP[1][0:MC[c], c * P:(c + 1) * P], ACT.Copy)
            ins.then_inc(S["wT"], 1)
            ac.wait_ge(S["wdrow_turned"], 1)
            nc.scalar.activation(wdrow[:], upP[:, 0, 0:C], ACT.Copy).then_inc(S["wdrow_ready"], 1)
            for t, s in pairs(ac):
                ac.wait_ge(S["turned"], t + 1)
                nc.scalar.activation(cols(xqT[:], t), turnP[s][:, 0:W], ACT.Copy).then_inc(S["xqT_ready"], 1)
            for t in turns(ac, N):
                for c, m in enumerate(MC):
                    ac.wait_ge(S["gate"], t * NC + c + 1)
                    wait(ac, S["hid_ready"], (t - 1) * NC + c + 1)
                    nc.scalar.activation(silu[0:m, c, :], gateP[0:m, c, :], ACT.Silu, scale=guscale[0:m, c:c + 1]
                                         ).then_inc(S["silu_ready"], 1)

        @block.tensor
        def _(pe):
            pe.wait_ge(S["id16"], 1)
            pe.wait_ge(S["w_q"], 1)
            for a in range(2):
                for c in range(NC):
                    ins = nc.tensor.transpose(turnP[0][:, (a * NC + c) * P:(a * NC + c + 1) * P], wguq[:, a, c, :], ident16[:])
            ins.then_inc(S["w_turned"], 1)
            for c, m in enumerate(MC):
                ins = nc.tensor.transpose(turnP[1][0:m, c * P:(c + 1) * P], wdq[:, c * P:c * P + m], ident16[:])
            ins.then_inc(S["w_turned"], 1)
            pe.wait_ge(S["diag_ready"], 1)
            nc.tensor.matmul(upP[:, 0, 0:C], ones[:], diag[:], start=True, stop=True).then_inc(S["wdrow_turned"], 1)
            pe.wait_ge(S["wT"], 2)
            for t, s in pairs(pe):
                pe.wait_ge(S["xq_ready"], t + 1)
                wait(pe, S["xqT_ready"], t - 1)
                for g in range(G):
                    ins = nc.tensor.transpose(turnP[s][:, g * P:(g + 1) * P], xqs[s][:, g, :], ident16[:])
                ins.then_inc(S["turned"], 1)
            pe.wait_ge(S["xqT_ready"], N)
            pe.wait_ge(S["wdrow_ready"], 1)
            for t in turns(pe, N):
                for c, m in enumerate(MC):
                    wait(pe, S["silu_ready"], (t - 1) * NC + c + 1)
                    nc.tensor.matmul(gateP[0:m, c, :], wguT[:, 0, c, 0:m], cols(xqT[:], t), start=True, stop=True
                                     ).then_inc(S["gate"], 1)
                    wait(pe, S["hid_ready"], (t - 1) * NC + c + 1)
                    nc.tensor.matmul(upP[0:m, c, :], wguT[:, 1, c, 0:m], cols(xqT[:], t), start=True, stop=True
                                     ).then_inc(S["up"], 1)
            for t, s in pairs(pe):
                pe.wait_ge(S["hq_ready"], t + 1)
                wait(pe, S["out_used"], t - 1)
                for g in range(G):
                    for c, m in enumerate(MC):
                        ins = nc.tensor.matmul(outP[s][:, g * C:(g + 1) * C], hq[s][0:m, c, g * P:(g + 1) * P], wdT[0:m, c, :],
                                               start=(c == 0), stop=(c == NC - 1))
                ins.then_inc(S["out"], 1)

        @block.vector
        def _(ve):
            st = Steps(ve, S["step"])
            st.begin(0)
            bc = lambda ap, shape: ap.to_broadcast(shape)
            ve.wait_ge(S["loaded"], 16 * LOADS)
            ve.wait_ge(S["filled"], 2)
            st.done(nc.vector.tensor_reduce(wmax[:, 0:2 * NC], wgu[:].rearrange("p a c h -> p (a c) h"), AX_X, ALU.max,
                                            apply_absolute_value=True))
            st.do(nc.vector.tensor_reduce(wmax[:, 2 * NC:], wd[:], AX_X, ALU.max, apply_absolute_value=True))
            st.do(nc.vector.tensor_scalar(wscale[:], wmax[:], 1.0 / QMAX, None, ALU.mult))
            st.do(nc.vector.reciprocal(winv[:], wscale[:]))
            for a in range(2):
                for c in range(NC):
                    st.done(nc.vector.tensor_scalar(wgu[:, a, c, :], wgu[:, a, c, :], winv[:, a * NC + c:a * NC + c + 1], QMAX,
                                                    ALU.mult, ALU.min))
            st.done(nc.vector.tensor_scalar(wd[:], wd[:], winv[:, 2 * NC:], QMAX, ALU.mult, ALU.min))
            st.sync()
            for b in (wgu, wd):
                st.done(nc.vector.tensor_scalar(b[:], b[:], -QMAX - 1.0, ROUND, ALU.max, ALU.add))
            st.sync()
            st.done(nc.vector.tensor_scalar(wguq[:], wgu[:], -ROUND, None, ALU.add))
            nc.vector.tensor_scalar(wdq[:], wd[:], -ROUND, None, ALU.add).then_inc(S["w_q"], 1)
            st.sync()
            nc.vector.tensor_scalar(diag[:], ident[:], wscale[:, 2 * NC:], None, ALU.mult).then_inc(S["diag_ready"], 1)

            for t in turns(ve, N):
                st.begin(t)
                norm.rows(nc, ve, st, t, lambda g: row(xres, t, g), lambda g: row(xn, t, g))
            st.begin(N)
            st.sync()
            nc.vector.tensor_reduce(xmax[:], xn[:], mybir.AxisListType.XY, ALU.max, apply_absolute_value=True
                                    ).then_inc(S["xmax_ready"], 1)

            def scales(k, everywhere):
                st.do(nc.vector.tensor_scalar(scale[:, k:k + 1], everywhere[:], sig[:, k:k + 1], 1.0 / QMAX, ALU.mult, ALU.mult))
                st.do(nc.vector.reciprocal(inv[:, k:k + 1], scale[:, k:k + 1]))

            ve.wait_ge(S["xall_ready"], 1)
            ve.wait_ge(S["sig_ready"], 1)
            scales(0, xall)
            st.do(nc.vector.tensor_scalar(guscale[:], wscale[:, 0:2 * NC], scale[:, 0:1], None, ALU.mult))
            st.do(nc.vector.tensor_scalar(xn[:], xn[:], inv[:, 0:1], QMAX, ALU.mult, ALU.min))
            st.do(nc.vector.tensor_scalar(xn[:], xn[:], -QMAX - 1.0, ROUND, ALU.max, ALU.add))
            for t, s in pairs(ve):
                wait(ve, S["turned"], t - 1)
                nc.vector.tensor_scalar(xqs[s], rows(xn, t), -ROUND, None, ALU.add).then_inc(S["xq_ready"], 1)

            for t in turns(ve, N):
                for c, m in enumerate(MC):
                    ve.wait_ge(S["up"], t * NC + c + 1)
                    ve.wait_ge(S["silu_ready"], t * NC + c + 1)
                    nc.vector.scalar_tensor_tensor(out=cols(hid[0:m, c, :], t), in0=upP[0:m, c, :],
                                                   scalar=guscale[0:m, NC + c:NC + c + 1], in1=silu[0:m, c, :],
                                                   op0=ALU.mult, op1=ALU.mult).then_inc(S["hid_ready"], 1)
            ve.wait_ge(S["hid_ready"], N * NC)
            for c, m in enumerate(MC):
                st.done(nc.vector.tensor_reduce(hmaxs[0:m, c:c + 1], hid[0:m, c, :], AX_X, ALU.max, apply_absolute_value=True))
            st.done(nc.vector.memset(hmaxs[MC[2]:P, 2:3], 0.0))
            st.sync()
            nc.vector.tensor_reduce(hmax[:], hmaxs[:, 0:NC], AX_X, ALU.max).then_inc(S["hmax_ready"], 1)
            ve.wait_ge(S["hall_ready"], 1)
            scales(1, hall)
            ve.wait_ge(S["wdrow_ready"], 1)
            st.do(nc.vector.tensor_scalar(wdrow[:], wdrow[:], scale[:, 1:2], None, ALU.mult))
            rest = Steps(ve, S["y_ready"])
            for t, s in pairs(ve):
                rest.begin(t)
                for c, m in enumerate(MC):
                    rest.done(nc.vector.tensor_scalar(cols(hid[0:m, c, :], t), cols(hid[0:m, c, :], t), inv[0:m, 1:2], QMAX,
                                                      ALU.mult, ALU.min))
                rest.sync()
                for c, m in enumerate(MC):
                    rest.done(nc.vector.tensor_scalar(cols(hid[0:m, c, :], t), cols(hid[0:m, c, :], t), -QMAX - 1.0, ROUND,
                                                      ALU.max, ALU.add))
                rest.sync()
                wait(ve, S["out"], t - 1)
                for c, m in enumerate(MC):
                    ins = nc.vector.tensor_scalar(hq[s][0:m, c, :], cols(hid[0:m, c, :], t), -ROUND, None, ALU.add)
                ins.then_inc(S["hq_ready"], 1)
                ve.wait_ge(S["out"], t + 1)
                nc.vector.tensor_tensor(y[:].rearrange("p (g c) -> p g c", g=G), outP[s].rearrange("p (g c) -> p g c", g=G),
                                        wdrow[:].unsqueeze(1).to_broadcast([P, G, C]), ALU.mult).then_inc(S["out_used"], 1)
                ve.wait_ge(S["out_used"], t + 1)
                rest.do(nc.vector.tensor_tensor(rows(xres, t), rows(xres, t), y[:].rearrange("p (g c) -> p g c", g=G), ALU.add))


def layout4(i, np):
    g = lambda n: i["L1_attn_" + n]
    return {"s4_win": g("w_in").T, "s4_wout": g("w_out").T.reshape(2, 64, C).transpose(1, 0, 2), "s4_wg": g("w_gate").T,
            "s4_bg": g("b_gate").reshape(1, C), "s4_ld": g("log_decay").reshape(64, 1), "s4_fr": g("frequency").reshape(64, 1),
            "s4_cpl": g("coupling"), "s4_w1": g("w_mlp1").T.reshape(C, 4, P), "s4_b1": g("b_mlp1").reshape(4, P).T,
            "s4_w2": g("w_mlp2").T.reshape(4, P, C).transpose(1, 0, 2), "s4_b2": g("b_mlp2").reshape(1, C),
            "s4_ln": np.stack([g("ln1_g"), g("ln1_b"), g("ln2_g"), g("ln2_b")], axis=1)}


def stage4(nc, xres, ident, dram):
    K = 64
    G = 4
    N = NT // G
    W = G * P
    CH = W // K
    ALLCH = NT * P // K
    BCH = L // K
    H = 4
    TWO_PI = 2.0 * math.pi
    ROUND = 1.5 * 2.0 ** 23
    PI1 = 201.0 / 32
    PI2 = 2029.0 / 2 ** 20
    PI3 = TWO_PI - PI1 - PI2
    with ExitStack() as ctx:
        sc = Scope(nc, ctx, "s4_")
        win = sc.sb("win", [P, 2, K])
        wout = sc.sb("wout", [K, 2, C])
        wg = sc.sb("wg", [P, C])
        bg = sc.sb("bg", [1, C])
        ld = sc.sb("ld", [K, 1])
        fr = sc.sb("fr", [K, 1])
        cpl = sc.sb("cpl", [K, K])
        w1 = sc.sb("w1", [P, H, P])
        b1 = sc.sb("b1", [P, H])
        w2 = sc.sb("w2", [P, H, C])
        b2 = sc.sb("b2", [1, C])
        ln = sc.sb("ln", [P, 4])
        ones = sc.sb("ones", [1, P])
        weff = sc.sb("weff", [K, 2, C])
        power = sc.sb("power", [K, K])
        magn = sc.sb("magn", [K, 1])
        magp = sc.sb("magp", [K, K])
        phase = sc.sb("phase", [K, K])
        turn = sc.sb("turn", [K, 2, K])
        ang = sc.sb("ang", [K, 2, K])
        trig = sc.sb("trig", [K, 2, K])
        table = sc.sb("table", [K, 3, 2 * K])
        mats = sc.sb("mats", [P, K, 2, K])
        hand = sc.sb("hand", [P, P])
        norm_a = Norm(sc, "na_", G)
        norm_b = Norm(sc, "nb_", G)
        cell = sc.sb("cell", [P, 2])
        seen = sc.sb("seen", [P, 1])
        x0 = sc.sb("x0", [P, NT, C])
        gate = sc.sb("gate", [P, NT, C])
        xn = [sc.sb(f"xn{s}", [P, G, C]) for s in range(2)]
        xT = [sc.sb(f"xT{s}", [P, W]) for s in range(2)]
        beta = sc.sb("beta", [P, ALLCH, K])
        carr = sc.sb("carr", [P, ALLCH, K])
        cs = sc.sb("cs", [P, CH, K])
        cT = sc.sb("cT", [K, 2, W])
        gh = sc.sb("gh", [P, G, C])
        x1 = sc.sb("x1", [P, G, C])
        act = sc.sb("act", [P, H, W])
        turnP = sc.ps("turnP", [P, W])
        hP = sc.ps("hP", [P, G, C])
        outP = sc.ps("outP", [P, G, C])
        cP = sc.ps("cP", [K, CH, 2, K])
        hidP = [sc.ps(f"hidP{s}", [P, W]) for s in range(2)]
        names = ("loaded", "blocks", "zeroed", "ones_ready", "powers", "mag_ready", "magp_ready", "ang_ready", "trig_ready", "table_ready",
                 "table_out", "mats_ready", "hand_ready", "weff_mm", "weff_ready", "step", "cell", "xn_ready",
                 "turned", "xT_ready", "beta_mm", "beta_ready", "gate_mm", "gate_ready", "states", "states_out",
                 "staged", "cturned", "cT_ready", "h_mm", "x1_ready", "n2_ready", "n2_turned", "x2T_ready",
                 "hidden", "acted", "out", "out_used", "pool_step")
        S = {n: sc.sem(n) for n in names}
        scratch = nc.dram_tensor("s4_scratch", (3, K, 2 * K), F32, kind="Internal").ap()
        block = ctx.enter_context(nc.Block())

        def pairs(eng):
            for j in turns(eng, N // 2):
                for s in range(2):
                    yield 2 * j + s, s

        def rows(buf, t, n=G):
            return buf[:, n * t:n * t + n, :] if isinstance(t, int) else buf[:, bass.ds(t * n, n), :]

        def row(buf, t, g):
            i = t * G + g
            return buf[:, i, :] if isinstance(i, int) else buf[:, bass.ds(i, 1), :]

        LOADS = 12

        @block.sync
        def _(sp):
            load_all(sp, S["loaded"], [(win[:].rearrange("p a k -> p (a k)"), dram["s4_win"]), (wout[:], dram["s4_wout"]),
                                       (wg[:], dram["s4_wg"]), (bg[:], dram["s4_bg"]), (ld[:], dram["s4_ld"]),
                                       (fr[:], dram["s4_fr"]), (w1[:], dram["s4_w1"]), (b1[:], dram["s4_b1"]),
                                       (w2[:], dram["s4_w2"]), (b2[:], dram["s4_b2"]), (ln[:], dram["s4_ln"])])
            sp.wait_ge(S["zeroed"], 2)
            for i in range(4):
                sp.dma_start(cpl[16 * i:16 * i + 16, 16 * i:16 * i + 16], dram["s4_cpl"][i]).then_inc(S["blocks"], 16)
            sp.wait_ge(S["table_ready"], 1)
            sp.dma_start(scratch.rearrange("q k i -> k q i"), table[:]).then_inc(S["table_out"], 16)
            sp.wait_ge(S["table_out"], 16)
            for part_in in range(2):
                for part_out in range(2):
                    q = (0, 1)[part_out] if part_in == 0 else (2, 0)[part_out]
                    src = bass.AP(tensor=scratch.tensor, offset=q * K * 2 * K, ap=[[1, K], [2 * K, K], [1, K]])
                    sp.dma_start(mats[part_in * K:part_in * K + K, :, part_out, :], src).then_inc(S["mats_ready"], 16)

        @block.gpsimd
        def _(pool):
            pool.memset(cpl[:], 0.0).then_inc(S["zeroed"], 1)
            pool.memset(table[:], 0.0).then_inc(S["zeroed"], 1)
            pool.memset(ones[:], 1.0).then_inc(S["ones_ready"], 1)
            pool.iota(power[:], pattern=[[1, K]], base=0, channel_multiplier=0,
                      allow_small_or_imprecise_dtypes=True).then_inc(S["powers"], 1)
            pool.memset(hand[:], 0.0).then_inc(S["hand_ready"], 1)
            for a in range(2):
                pool.wait_ge(S["hand_ready"], a + 1)
                at = a * K + K - 1
                pool.affine_select(out=hand[:], in_=hand[:], compare_op=ALU.not_equal, fill=1.0, base=-257 * at,
                                   pattern=[[1, P]], channel_multiplier=256).then_inc(S["hand_ready"], 1)
            norm_a.setup(pool)
            norm_b.setup(pool)
            pool.wait_ge(S["powers"], 1)
            pool.wait_ge(S["mag_ready"], 1)
            nc.gpsimd.tensor_tensor(magp[:], magn[:].to_broadcast([K, K]), power[:], ALU.pow).then_inc(S["magp_ready"], 1)
            for t in turns(pool, N):
                norm_a.root(nc, pool, t)
                norm_b.root(nc, pool, t)

            def stage_in(t):
                wait(pool, S["cturned"], t)
                part = carr[:, t * CH:t * CH + CH, :] if isinstance(t, int) else carr[:, bass.ds(t * CH, CH), :]
                st.hold(cell)
                nc.gpsimd.tensor_copy(cs[:], part).then_inc(S["staged"], 1)

            st = Steps(pool, S["pool_step"])
            st.begin(0)
            st.done(nc.gpsimd.memset(cell[:], 0.0))
            pool.wait_ge(S["states_out"], 8)
            stage_in(0)
            norm_b.root(nc, pool, N)
            for t in turns(pool, N, last=1):
                st.begin(t)
                if not (isinstance(t, int) and t == N - 1):
                    stage_in(t + 1)
                    norm_b.root(nc, pool, t + 1 + N)

        @block.scalar
        def _(ac):
            ac.wait_ge(S["loaded"], 16 * (LOADS - 1))
            nc.scalar.activation(magn[:], ld[:], ACT.Sigmoid).then_inc(S["mag_ready"], 1)
            ac.wait_ge(S["ang_ready"], 1)
            nc.scalar.activation(trig[:], ang[:], ACT.Sin).then_inc(S["trig_ready"], 1)
            ac.wait_ge(S["weff_mm"], 1)
            nc.scalar.activation(weff[:], hP[0:K, 0:2, :], ACT.Copy).then_inc(S["weff_ready"], 1)
            for t, s in pairs(ac):
                ac.wait_ge(S["turned"], t + 1)
                wait(ac, S["gate_mm"], t - 1)
                nc.scalar.activation(xT[s][:], turnP[:], ACT.Identity, scale=ln[:, 0:1], bias=ln[:, 1:2]
                                     ).then_inc(S["xT_ready"], 1)
                ac.wait_ge(S["beta_mm"], t + 1)
                dst = beta[:, t * CH:t * CH + CH, :] if isinstance(t, int) else beta[:, bass.ds(t * CH, CH), :]
                nc.scalar.activation(dst, outP[:].rearrange("p g c -> p (g c)").rearrange("p (n k) -> p n k", k=K), ACT.Copy
                                     ).then_inc(S["beta_ready"], 1)
                ac.wait_ge(S["gate_mm"], t + 1)
                nc.scalar.activation(rows(gate, t), hP[:], ACT.Sigmoid).then_inc(S["gate_ready"], 1)
            for i in range(8):
                ac.wait_ge(S["states"], i + 1)
                nc.scalar.activation(carr[:, :, 8 * i:8 * i + 8], hidP[i % 2][:].rearrange("p (n k) -> p n k", k=8), ACT.Copy
                                     ).then_inc(S["states_out"], 1)

            def back(t):
                ac.wait_ge(S["cturned"], t + 1)
                wait(ac, S["h_mm"], t)
                for a in range(2):
                    ins = nc.scalar.activation(cT[:, a, :].rearrange("k (n j) -> k n j", j=K), cP[:, :, a, ::-1], ACT.Copy)
                ins.then_inc(S["cT_ready"], 1)

            def turn_in(t):
                ac.wait_ge(S["n2_turned"], t + 1)
                wait(ac, S["hidden"], t * H)
                nc.scalar.activation(xT[0][:], turnP[:], ACT.Identity, scale=ln[:, 2:3], bias=ln[:, 3:4]
                                     ).then_inc(S["x2T_ready"], 1)

            back(0)
            turn_in(0)
            for t in turns(ac, N, last=1):
                for c in range(H):
                    ac.wait_ge(S["hidden"], t * H + c + 1)
                    if c == 0:
                        wait(ac, S["out"], t)
                    nc.scalar.activation(act[:, c, :], hidP[c % 2][:], ACT.Silu, bias=b1[:, c:c + 1]).then_inc(S["acted"], 1)
                if not (isinstance(t, int) and t == N - 1):
                    back(t + 1)
                    turn_in(t + 1)

        @block.tensor
        def _(pe):
            pe.wait_ge(S["loaded"], 16 * (LOADS - 1))
            pe.wait_ge(S["blocks"], 64)
            for a in range(2):
                ins = nc.tensor.matmul(hP[0:K, a, :], cpl[:], wout[:, a, :], start=True, stop=True)
            ins.then_inc(S["weff_mm"], 1)
            pe.wait_ge(S["ones_ready"], 1)
            pe.wait_ge(S["weff_ready"], 1)
            for t, s in pairs(pe):
                pe.wait_ge(S["xn_ready"], t + 1)
                wait(pe, S["xT_ready"], t)
                for g in range(G):
                    ins = nc.tensor.transpose(turnP[:, g * P:(g + 1) * P], xn[s][:, g, :], ident[:])
                ins.then_inc(S["turned"], 1)
                pe.wait_ge(S["xT_ready"], t + 1)
                wait(pe, S["beta_ready"], t)
                flat = outP[:].rearrange("p g c -> p (g c)")
                for a in range(2):
                    for n in range(CH):
                        ins = nc.tensor.matmul(flat[a * K:a * K + K, n * K:n * K + K], xT[s][:, n * K:n * K + K], win[:, a, :],
                                               start=True, stop=True)
                ins.then_inc(S["beta_mm"], 1)
                wait(pe, S["gate_ready"], t)
                for g in range(G):
                    nc.tensor.matmul(hP[:, g, :], ones[:], bg[:], start=True, stop=False)
                    ins = nc.tensor.matmul(hP[:, g, :], xT[s][:, g * P:g * P + P], wg[:], start=False, stop=True)
                ins.then_inc(S["gate_mm"], 1)
            pe.wait_ge(S["beta_ready"], N)
            pe.wait_ge(S["mats_ready"], 64)
            pe.wait_ge(S["hand_ready"], 3)
            by_batch = beta[:].rearrange("p (b n) k -> p b n k", n=BCH)
            for i in range(8):
                wait(pe, S["states_out"], i - 1)
                dst = hidP[i % 2][:].rearrange("p (b n k) -> p b n k", n=BCH, k=8)
                for k in range(8):
                    nc.tensor.matmul(dst[:, :, :, k], mats[:, 8 * i + k].rearrange("p a j -> p (a j)"),
                                     by_batch[:, :, :, 8 * i + k], start=(k == 0), stop=False, skip_group_check=True)
                for n in range(1, BCH):
                    ins = nc.tensor.matmul(dst[:, :, n, :], hand[:], by_batch[:, :, n - 1, 8 * i:8 * i + 8], start=False,
                                           stop=(n == BCH - 1), skip_group_check=True)
                ins.then_inc(S["states"], 1)

            def front1(t):
                pe.wait_ge(S["staged"], t + 1)
                wait(pe, S["cT_ready"], t)
                nc.tensor.matmul(cP[0:32, 0, 0, 0:1], ident[:, 0:32], ident[:, 0:1], start=True, stop=True)
                for n in range(CH):
                    ins = nc.tensor.transpose(cP[:, n].rearrange("k a j -> k (a j)"), cs[:, n, :], ident[:])
                ins.then_inc(S["cturned"], 1)
                pe.wait_ge(S["cT_ready"], t + 1)
                wait(pe, S["x1_ready"], t)
                for g in range(G):
                    for a in range(2):
                        ins = nc.tensor.matmul(hP[:, g, :], cT[:, a, g * P:g * P + P], weff[:, a, :], start=(a == 0), stop=(a == 1))
                ins.then_inc(S["h_mm"], 1)

            def front2(t):
                pe.wait_ge(S["n2_ready"], t + 1)
                wait(pe, S["x2T_ready"], t)
                for g in range(G):
                    ins = nc.tensor.transpose(turnP[:, g * P:(g + 1) * P], xn[0][:, g, :], ident[:])
                ins.then_inc(S["n2_turned"], 1)

            front1(0)
            front2(0)
            for t in turns(pe, N, last=1):
                more = not (isinstance(t, int) and t == N - 1)
                pe.wait_ge(S["x2T_ready"], t + 1)
                for c in range(H):
                    wait(pe, S["acted"], t * H + c - 1)
                    nc.tensor.matmul(hidP[c % 2][:], w1[:, c, :], xT[0][:], start=True, stop=True).then_inc(S["hidden"], 1)
                if more:
                    front1(t + 1)
                pe.wait_ge(S["acted"], t * H + H)
                wait(pe, S["out_used"], t)
                for g in range(G):
                    nc.tensor.matmul(outP[:, g, :], ones[:], b2[:], start=True, stop=False)
                    for c in range(H):
                        ins = nc.tensor.matmul(outP[:, g, :], act[:, c, g * P:g * P + P], w2[:, c, :], start=False, stop=(c == H - 1))
                ins.then_inc(S["out"], 1)
                if more:
                    front2(t + 1)

        @block.vector
        def _(ve):
            st = Steps(ve, S["step"])
            st.begin(0)
            ve.wait_ge(S["powers"], 1)
            ve.wait_ge(S["loaded"], 16 * (LOADS - 1))
            st.do(nc.vector.tensor_scalar(phase[:], power[:], fr[:, 0:1], None, ALU.mult))
            for a in range(2):
                st.do(nc.vector.tensor_scalar(turn[:, a, :], phase[:], 1.0 / TWO_PI, 0.25 * (1 - a), ALU.mult, ALU.add))
            st.do(nc.vector.tensor_scalar(turn[:], turn[:], ROUND, -ROUND, ALU.add, ALU.add))
            for a in range(2):
                st.do(nc.vector.scalar_tensor_tensor(out=ang[:, a, :], in0=turn[:, a, :], scalar=-PI1, in1=phase[:], op0=ALU.mult, op1=ALU.add))
            for part in (PI2, PI3):
                st.do(nc.vector.scalar_tensor_tensor(out=ang[:], in0=turn[:], scalar=-part, in1=ang[:], op0=ALU.mult, op1=ALU.add))
            st.do(nc.vector.tensor_scalar(ang[:, 0, :], ang[:, 0, :], math.pi / 2, None, ALU.add))
            nc.vector.tensor_scalar(ang[:], ang[:], 3.1415925, -3.1415925, ALU.min, ALU.max).then_inc(S["ang_ready"], 1)
            ve.wait_ge(S["trig_ready"], 1)
            ve.wait_ge(S["magp_ready"], 1)
            ve.wait_ge(S["zeroed"], 2)
            for q in range(2):
                st.done(nc.vector.tensor_tensor(table[:, q, K - 1:2 * K - 1], trig[:, q, :], magp[:], ALU.mult))
            st.sync()
            st.done(nc.vector.memset(table[:, 0, K - 1:K], 1.0))
            st.done(nc.vector.memset(table[:, 1, K - 1:K], 0.0))
            st.sync()
            nc.vector.tensor_scalar(table[:, 2, :], table[:, 1, :], -1.0, None, ALU.mult).then_inc(S["table_ready"], 1)

            for t, s in pairs(ve):
                st.begin(t)
                norm_a.rows(nc, ve, st, t, lambda g: row(xres, t, g), lambda g: row(x0, t, g))
                st.sync()
                wait(ve, S["turned"], t - 1)
                norm_b.rows(nc, ve, st, t, lambda g: row(x0, t, g), lambda g: xn[s][:, g, :])
                st.sync()
                nc.vector.tensor_copy(seen[:], xn[s][:, 0, 0:1]).then_inc(S["xn_ready"], 1)

            rest = Steps(ve, S["cell"])
            rest.begin(0)

            def front(t, s):
                ve.wait_ge(S["h_mm"], t + 1)
                rest.do(nc.vector.tensor_tensor(gh[:], hP[:], rows(gate, t), ALU.mult))
                nc.vector.tensor_tensor(x1[:], gh[:], rows(x0, t), ALU.add).then_inc(S["x1_ready"], 1)
                ve.wait_ge(S["x1_ready"], t + 1)
                rest.done(nc.vector.tensor_tensor(rows(xres, t), rows(xres, t), x1[:], ALU.add))
                wait(ve, S["n2_turned"], t)
                norm_b.rows(nc, ve, rest, t + N, lambda g: x1[:, g, :], lambda g: xn[0][:, g, :])
                rest.sync()
                nc.vector.tensor_copy(seen[:], xn[0][:, 0, 0:1]).then_inc(S["n2_ready"], 1)

            ve.wait_ge(S["gate_ready"], N)
            ve.wait_ge(S["turned"], N)
            front(0, 0)
            for t in turns(ve, N, last=1):
                rest.begin(t)
                if not (isinstance(t, int) and t == N - 1):
                    front(t + 1, 0)
                ve.wait_ge(S["out"], t + 1)
                nc.vector.tensor_tensor(rows(xres, t), rows(xres, t), outP[:], ALU.add).then_inc(S["out_used"], 1)


def layout5(i, np):
    g = lambda n: i["L1_xattn_" + n]
    laid = {"ctx": i["ctx_512"].reshape(8, P, 64).transpose(1, 0, 2)}
    for n in ("ln1_g", "ln1_b", "ln2_g", "ln2_b"):
        laid["s5" + n] = g(n).reshape(1, C)
    for tag, a in (("s5a_", "a1_"), ("s5c_", "a2_")):
        w = lambda n: g(a + n)
        heads = lambda n: w(n).transpose(1, 0, 2)
        laid.update({tag + "wq": heads("wq").reshape(C, 4, P), tag + "wk": heads("wk").reshape(-1, 4, P),
                     tag + "wv": heads("wv").reshape(-1, 512), tag + "wo": w("li1_w").reshape(4, P, C).transpose(1, 0, 2),
                     tag + "bo": w("li1_b").reshape(1, C), tag + "w1": w("li2_w").reshape(C, 4, P),
                     tag + "b1": w("li2_b").reshape(4, P).T, tag + "w2": w("li3_w").reshape(4, P, C).transpose(1, 0, 2),
                     tag + "b2": w("li3_b").reshape(1, C)})
    w = lambda n: g("a1_" + n)
    laid["s5a_ln"] = np.stack([w("lnx_g"), w("lnx_b"), w("lny_g"), w("lny_b")], axis=1)
    w3 = lambda a: np.stack([g(a + "ln3_g"), g(a + "ln3_b")], axis=1)
    laid["s5m_ln"], laid["s5n_ln"] = w3("a1_"), w3("a2_")
    for m, a in (("s5m_", "s5a_"), ("s5n_", "s5c_")):
        for n in ("w1", "b1", "w2", "b2"):
            laid[m + n] = laid.pop(a + n)
    w = lambda n: g("a2_" + n)
    laid["s5c_ln"] = np.stack([w("lnx_g"), w("lnx_b"), w("lnx_g"), w("lnx_b")], axis=1)
    laid["s5c_cln"] = np.stack([w("lny_g"), w("lny_b")], axis=1)
    return laid


def stage5(nc, xres, ident, dram):
    with ExitStack() as ctx:
        sc = Scope(nc, ctx, "s5_")
        hat = sc.sb("hat", [P, NT, C])
        x = sc.sb("x", [P, NT, C])
        xo = sc.sb("xo", [P, NT, C])
        normalise(nc, "n5a_", xres, hat, affine=(dram["s5ln1_g"], dram["s5ln1_b"]), dst=x, twice=True)
        attend(nc, xres, ident, dram, "s5a_", hat, x, xo, "after", 32, True, False, False)
        mlp(nc, xres, ident, dram, "s5m_", xo, x)
        normalise(nc, "n5b_", x, hat, affine=(dram["s5ln2_g"], dram["s5ln2_b"]), add_to=xres, dst=x)
        attend(nc, xres, ident, dram, "s5c_", hat, x, xo, "cross", 32, True, False, True)
        mlp(nc, xres, ident, dram, "s5n_", xo, xres)


def layout6(i, np):
    w1 = i["L1_ffn_W1"].reshape(8, 2, 2, P, C)
    return {"m6_w1": w1.transpose(4, 0, 2, 1, 3).reshape(C, 8, 4, P),
            "m6_w2": i["L1_ffn_W2"].reshape(8, C, 2, P).transpose(3, 0, 2, 1),
            "m6_wr": i["L1_ffn_Wr"].T}


def stage6(nc, xres, ident, dram):
    mixture(nc, xres, ident, dram, "m6_", 8, 4, True)


def lay_out(i, np):
    laid = {"x": i["x"].reshape(NB * L, C)}
    laid.update(layout1(i, np))
    laid.update(layout2(i, np))
    laid.update(layout3(i, np))
    laid.update(layout4(i, np))
    laid.update(layout5(i, np))
    laid.update(layout6(i, np))
    return laid


NEEDED = None
STAGES = [stage1, stage2, stage3, stage4, stage5, stage6]


def build(nc, dram, out):
    with ExitStack() as ctx:
        sc = Scope(nc, ctx, "")
        xres = sc.sb("xres", [P, NT, C])
        ident = sc.sb("ident", [P, P])
        came = sc.sem("came")
        ready = sc.sem("ready")
        gone = sc.sem("gone")
        with nc.Block() as block:
            @block.sync
            def _(sp):
                sp.dma_start(xres[:], dram["x"].rearrange("(t p) c -> p t c", p=P)).then_inc(came, 16)
                sp.wait_ge(came, 16)

            @block.gpsimd
            def _(pool):
                identity(nc, pool, ident[:], ready)

        for stage in STAGES:
            stage(nc, xres, ident, dram)

        with nc.Block() as block:
            @block.sync
            def _(sp):
                sp.dma_start(out.rearrange("(t p) c -> p t c", p=P), xres[:]).then_inc(gone, 16)
                sp.wait_ge(gone, 16)


def kernel(**inputs):
    import numpy as np
    import concourse.bacc as bacc
    from concourse.bass_utils import run_bass_kernel_spmd

    laid = lay_out({k: np.asarray(v) for k, v in inputs.items() if NEEDED is None or k in NEEDED}, np)
    nc = bacc.Bacc("TRN2", target_bir_lowering=False, num_devices=1)
    arrays, dram = {}, {}
    for name, a in laid.items():
        a = np.ascontiguousarray(a)
        arrays["in_" + name] = a
        dram[name] = nc.dram_tensor("in_" + name, a.shape, mybir.dt.from_np(a.dtype), kind="ExternalInput").ap()
    out = nc.dram_tensor("out", (NB * L, C), F32, kind="ExternalOutput").ap()
    build(nc, dram, out)
    r = run_bass_kernel_spmd(nc, [arrays], core_ids=[0])
    return r.results[0]["out"].reshape(NB, L, C)
```
